# Optimizing a Trainium2 kernel written in Bass

```python
import numpy as np
import jax
import jax.numpy as jnp

def _softmax(x, axis=-1):
    return jax.nn.softmax(x, axis=axis)

def _gelu(x):
    return jax.nn.gelu(x, approximate=True)

def _silu(x):
    return jax.nn.silu(x)

def _sigmoid(x):
    return jax.nn.sigmoid(x)

def _layernorm(x, axis=-1, eps=1e-05):
    m = jnp.mean(x, axis=axis, keepdims=True)
    v = jnp.var(x, axis=axis, keepdims=True)
    return (x - m) / jnp.sqrt(v + eps)

def _scatter_add(tgt, idx, src, axis=0):
    return tgt.at[idx].add(src)

def _segment_sum(src, seg, n):
    return jax.ops.segment_sum(src, seg, n)
kernel_name = 'mk_macaron_d2_jaxref_r8_ca16bf'

def setup_inputs(seed: int=0):
    np.random.seed(seed)
    _w = jnp.asarray

    def _L0_attn_setup():
        import jax, jax.numpy as jnp
        import numpy as np
        B, S, D_IN = (2, 256, 128)
        D_OUT, H, WINDOW = (128, 16, 64)
        HD = D_OUT // H
        key = jax.random.key(seed)
        k1, k2, k3, k4 = jax.random.split(key, 4)
        scale_in = 1.0 / np.sqrt(D_IN)
        scale_out = 1.0 / np.sqrt(D_OUT)
        return {'x': jax.random.normal(k1, (B, S, D_IN), dtype=jnp.float32), 'w_qkv': jax.random.normal(k2, (3 * D_OUT, D_IN), dtype=jnp.float32) * scale_in, 'w_out': jax.random.normal(k3, (D_OUT, D_OUT), dtype=jnp.float32) * scale_out, 'b_out': jax.random.normal(k4, (D_OUT,), dtype=jnp.float32) * scale_out}
    _L0_attn_in = _L0_attn_setup()

    def _L0_ffn_setup():
        import jax, jax.numpy as jnp
        import numpy as np
        B, T, D = (1, 256, 128)
        E, DFF = (8, 512)

        def _gating(logits):
            S, num_e = logits.shape
            gates = jax.nn.softmax(logits.astype(jnp.float32), axis=1)
            idx1 = jnp.argmax(gates, axis=1)
            mask1 = jax.nn.one_hot(idx1, num_e, dtype=jnp.int32)
            logits_ex1 = jnp.where(mask1.astype(bool), -jnp.inf, logits)
            idx2 = jnp.argmax(logits_ex1, axis=1)
            mask2 = jax.nn.one_hot(idx2, num_e, dtype=jnp.int32)
            loc1 = jnp.cumsum(mask1, axis=0) - 1
            loc2 = jnp.cumsum(mask2, axis=0) - 1 + jnp.sum(mask1, axis=0, keepdims=True)
            loc1_s = jnp.sum(loc1 * mask1, axis=1)
            loc2_s = jnp.sum(loc2 * mask2, axis=1)
            g1 = jnp.sum(gates * mask1, axis=1)
            g2 = jnp.sum(gates * mask2, axis=1)
            denom = jnp.maximum(g1 + g2, jnp.finfo(jnp.float32).eps)
            g1, g2 = (g1 / denom, g2 / denom)
            cap = S
            loc1_sc = jax.nn.one_hot(loc1_s, cap, dtype=jnp.float32)
            loc2_sc = jax.nn.one_hot(loc2_s, cap, dtype=jnp.float32)
            combine = (g1[:, None] * mask1)[:, :, None] * loc1_sc[:, None, :] + (g2[:, None] * mask2)[:, :, None] * loc2_sc[:, None, :]
            dispatch_mask = combine != 0
            return (combine.astype(logits.dtype), dispatch_mask)
        key = jax.random.key(seed)
        k1, k2, k3, k4 = jax.random.split(key, 4)
        x = jax.random.normal(k1, (B, T, D), dtype=jnp.float32)
        Wg = jax.random.normal(k2, (D, E), dtype=jnp.float32) * (1.0 / np.sqrt(D))
        w1 = jax.random.normal(k3, (D, DFF), dtype=jnp.float32) * (1.0 / np.sqrt(D))
        w2 = jax.random.normal(k4, (DFF, D), dtype=jnp.float32) * (1.0 / np.sqrt(DFF))
        return {'x': x, 'Wg': Wg, 'w1': w1, 'w2': w2}
    _L0_ffn_in = _L0_ffn_setup()

    def _L1_attn_setup():
        import jax, jax.numpy as jnp
        import numpy as np
        from jax import lax
        D_MODEL = 128
        D_STATE = 16
        D_CONV = 4
        EXPAND = 2
        D_INNER = EXPAND * D_MODEL
        DT_RANK = -(-D_MODEL // 16)
        B, L = (2, 128)

        def _selective_scan(u, delta, a, b, c):
            deltaA = jnp.exp(jnp.einsum('bld,dn->bldn', delta, a))
            deltaBu = jnp.einsum('bld,bln,bld->bldn', delta, b, u)

            def step(h, inp):
                dA_t, dBu_t, c_t = inp
                h = dA_t * h + dBu_t
                y = jnp.einsum('bdn,bn->bd', h, c_t)
                return (h, y)
            h0 = jnp.zeros((u.shape[0], u.shape[2], a.shape[1]), dtype=u.dtype)
            xs = (jnp.moveaxis(deltaA, 1, 0), jnp.moveaxis(deltaBu, 1, 0), jnp.moveaxis(c, 1, 0))
            _, ys = lax.scan(step, h0, xs)
            return jnp.moveaxis(ys, 0, 1)
        key = jax.random.key(seed)
        ks = jax.random.split(key, 10)
        s = 0.02
        x = jax.random.normal(ks[0], (B, L, D_MODEL), dtype=jnp.float32)
        in_proj_w = jax.random.normal(ks[1], (2 * D_INNER, D_MODEL), dtype=jnp.float32) * s
        in_proj_b = jnp.zeros((2 * D_INNER,), dtype=jnp.float32)
        conv_w = jax.random.normal(ks[2], (D_INNER, 1, D_CONV), dtype=jnp.float32) * 0.1
        conv_b = jnp.zeros((D_INNER,), dtype=jnp.float32)
        x_proj_w = jax.random.normal(ks[3], (DT_RANK + 2 * D_STATE, D_INNER), dtype=jnp.float32) * s
        dt_proj_w = jax.random.normal(ks[4], (D_INNER, DT_RANK), dtype=jnp.float32) * s
        dt_proj_b = jnp.zeros((D_INNER,), dtype=jnp.float32)
        A_log = jnp.log(jnp.broadcast_to(jnp.arange(1, D_STATE + 1, dtype=jnp.float32), (D_INNER, D_STATE)))
        D_param = jnp.ones((D_INNER,), dtype=jnp.float32)
        out_proj_w = jax.random.normal(ks[5], (D_MODEL, D_INNER), dtype=jnp.float32) * s
        out_proj_b = jnp.zeros((D_MODEL,), dtype=jnp.float32)
        return dict(x=x, in_proj_w=in_proj_w, in_proj_b=in_proj_b, conv_w=conv_w, conv_b=conv_b, x_proj_w=x_proj_w, dt_proj_w=dt_proj_w, dt_proj_b=dt_proj_b, A_log=A_log, D_param=D_param, out_proj_w=out_proj_w, out_proj_b=out_proj_b)
    _L1_attn_in = _L1_attn_setup()

    def _L1_ffn_setup():
        import jax, jax.numpy as jnp
        import numpy as np
        EPS = 1e-08

        def _ternary_linear(x, w):
            alpha = jnp.mean(jnp.abs(w))
            w_t = jnp.sign(w) * (jnp.abs(w) > 0.5 * alpha).astype(w.dtype)
            w_q = w + jax.lax.stop_gradient(w_t - w)
            d = x.shape[-1]
            rms = jnp.sqrt(jnp.sum(x * x, axis=-1, keepdims=True)) / jnp.sqrt(jnp.asarray(d, x.dtype))
            x_norm = x / (rms + EPS)
            return jnp.einsum('bsd,fd->bsf', x_norm, w_q)
        key = jax.random.key(seed)
        k1, k2, k3 = jax.random.split(key, 3)
        d_model, d_ff = (128, 512)
        B, S = (4, 512)
        x = jax.random.normal(k1, (B, S, d_model), dtype=jnp.float32)
        w_up = jax.random.normal(k2, (d_ff, d_model), dtype=jnp.float32) * 0.02
        w_down = jax.random.normal(k3, (d_model, d_ff), dtype=jnp.float32) * 0.02
        return {'x': x, 'w_up': w_up, 'w_down': w_down}
    _L1_ffn_in = _L1_ffn_setup()
    _d = {'L0_attn_x': _L0_attn_in['x'], 'L0_attn_w_qkv': _L0_attn_in['w_qkv'], 'L0_attn_w_out': _L0_attn_in['w_out'], 'L0_attn_b_out': _L0_attn_in['b_out'], 'L0_ffn_Wg': _L0_ffn_in['Wg'], 'L0_ffn_w1': _L0_ffn_in['w1'], 'L0_ffn_w2': _L0_ffn_in['w2'], 'L1_attn_in_proj_w': _L1_attn_in['in_proj_w'], 'L1_attn_in_proj_b': _L1_attn_in['in_proj_b'], 'L1_attn_conv_w': _L1_attn_in['conv_w'], 'L1_attn_conv_b': _L1_attn_in['conv_b'], 'L1_attn_x_proj_w': _L1_attn_in['x_proj_w'], 'L1_attn_dt_proj_w': _L1_attn_in['dt_proj_w'], 'L1_attn_dt_proj_b': _L1_attn_in['dt_proj_b'], 'L1_attn_A_log': _L1_attn_in['A_log'], 'L1_attn_D_param': _L1_attn_in['D_param'], 'L1_attn_out_proj_w': _L1_attn_in['out_proj_w'], 'L1_attn_out_proj_b': _L1_attn_in['out_proj_b'], 'L1_ffn_w_up': _L1_ffn_in['w_up'], 'L1_ffn_w_down': _L1_ffn_in['w_down']}
    _x0 = _d['L0_attn_x']
    _d['L0_attn_x'] = jax.random.normal(jax.random.fold_in(jax.random.key(seed), 1), (2, 1024, 128), dtype=_x0.dtype)
    del _x0
    return _d

def reference(L0_attn_x, L0_attn_w_qkv, L0_attn_w_out, L0_attn_b_out, L0_ffn_Wg, L0_ffn_w1, L0_ffn_w2, L1_attn_in_proj_w, L1_attn_in_proj_b, L1_attn_conv_w, L1_attn_conv_b, L1_attn_x_proj_w, L1_attn_dt_proj_w, L1_attn_dt_proj_b, L1_attn_A_log, L1_attn_D_param, L1_attn_out_proj_w, L1_attn_out_proj_b, L1_ffn_w_up, L1_ffn_w_down):

    def _L0_attn_ref(x, w_qkv, w_out, b_out):
        import jax, jax.numpy as jnp
        import numpy as np
        B, S, D_IN = (2, 256, 128)
        D_OUT, H, WINDOW = (128, 16, 64)
        HD = D_OUT // H
        b, s, _ = x.shape
        qkv = jnp.einsum('bsi,oi->bso', x, w_qkv)
        q, k, v = jnp.split(qkv, 3, axis=-1)

        def heads(t):
            return t.reshape(b, s, H, HD).transpose(0, 2, 1, 3)
        q, k, v = (heads(q), heads(k), heads(v))
        scores = jnp.einsum('bhqd,bhkd->bhqk', q, k) / jnp.sqrt(jnp.asarray(HD, x.dtype))
        i = jnp.arange(s)[:, None]
        j = jnp.arange(s)[None, :]
        allowed = (j <= i) & (i - j < WINDOW)
        scores = jnp.where(allowed[None, None], scores, jnp.asarray(-jnp.inf, x.dtype))
        attn = jax.nn.softmax(scores, axis=-1)
        ctx = jnp.einsum('bhqk,bhkd->bhqd', attn, v)
        ctx = ctx.transpose(0, 2, 1, 3).reshape(b, s, D_OUT)
        return jnp.einsum('bso,po->bsp', ctx, w_out) + b_out

    def _L0_ffn_ref(x, Wg, w1, w2):
        import jax, jax.numpy as jnp
        import numpy as np
        B, T, D = (1, 256, 128)
        E, DFF = (8, 512)

        def _gating(logits):
            S, num_e = logits.shape
            gates = jax.nn.softmax(logits.astype(jnp.float32), axis=1)
            idx1 = jnp.argmax(gates, axis=1)
            mask1 = jax.nn.one_hot(idx1, num_e, dtype=jnp.int32)
            logits_ex1 = jnp.where(mask1.astype(bool), -jnp.inf, logits)
            idx2 = jnp.argmax(logits_ex1, axis=1)
            mask2 = jax.nn.one_hot(idx2, num_e, dtype=jnp.int32)
            loc1 = jnp.cumsum(mask1, axis=0) - 1
            loc2 = jnp.cumsum(mask2, axis=0) - 1 + jnp.sum(mask1, axis=0, keepdims=True)
            loc1_s = jnp.sum(loc1 * mask1, axis=1)
            loc2_s = jnp.sum(loc2 * mask2, axis=1)
            g1 = jnp.sum(gates * mask1, axis=1)
            g2 = jnp.sum(gates * mask2, axis=1)
            denom = jnp.maximum(g1 + g2, jnp.finfo(jnp.float32).eps)
            g1, g2 = (g1 / denom, g2 / denom)
            cap = S
            loc1_sc = jax.nn.one_hot(loc1_s, cap, dtype=jnp.float32)
            loc2_sc = jax.nn.one_hot(loc2_s, cap, dtype=jnp.float32)
            combine = (g1[:, None] * mask1)[:, :, None] * loc1_sc[:, None, :] + (g2[:, None] * mask2)[:, :, None] * loc2_sc[:, None, :]
            dispatch_mask = combine != 0
            return (combine.astype(logits.dtype), dispatch_mask)
        d_model = x.shape[2]
        xs = x.reshape(-1, d_model)
        logits = xs @ Wg
        combine, dispatch_mask = _gating(logits)
        dispatched = jnp.einsum('sec,sm->ecm', dispatch_mask.astype(jnp.float32), xs)
        expert_out = jax.nn.relu(dispatched @ w1) @ w2
        out = jnp.einsum('sec,ecm->sm', combine, expert_out)
        return out.reshape(x.shape)

    def _L1_attn_ref(x, in_proj_w, in_proj_b, conv_w, conv_b, x_proj_w, dt_proj_w, dt_proj_b, A_log, D_param, out_proj_w, out_proj_b):
        import jax, jax.numpy as jnp
        import numpy as np
        from jax import lax
        D_MODEL = 128
        D_STATE = 16
        D_CONV = 4
        EXPAND = 2
        D_INNER = EXPAND * D_MODEL
        DT_RANK = -(-D_MODEL // 16)
        B, L = (2, 128)

        def _selective_scan(u, delta, a, b, c):
            deltaA = jnp.exp(jnp.einsum('bld,dn->bldn', delta, a))
            deltaBu = jnp.einsum('bld,bln,bld->bldn', delta, b, u)

            def step(h, inp):
                dA_t, dBu_t, c_t = inp
                h = dA_t * h + dBu_t
                y = jnp.einsum('bdn,bn->bd', h, c_t)
                return (h, y)
            h0 = jnp.zeros((u.shape[0], u.shape[2], a.shape[1]), dtype=u.dtype)
            xs = (jnp.moveaxis(deltaA, 1, 0), jnp.moveaxis(deltaBu, 1, 0), jnp.moveaxis(c, 1, 0))
            _, ys = lax.scan(step, h0, xs)
            return jnp.moveaxis(ys, 0, 1)
        x_and_res = x @ in_proj_w.T + in_proj_b
        x_b, res = jnp.split(x_and_res, [D_INNER], axis=-1)
        xc = jnp.transpose(x_b, (0, 2, 1))
        xc = lax.conv_general_dilated(xc, conv_w, window_strides=(1,), padding=[(D_CONV - 1, 0)], dimension_numbers=('NCH', 'OIH', 'NCH'), feature_group_count=D_INNER)
        xc = xc + conv_b[None, :, None]
        x_b = jax.nn.silu(jnp.transpose(xc, (0, 2, 1)))
        x_dbl = x_b @ x_proj_w.T
        delta, b, c = jnp.split(x_dbl, [DT_RANK, DT_RANK + D_STATE], axis=-1)
        delta = jax.nn.softplus(delta @ dt_proj_w.T + dt_proj_b)
        a = -jnp.exp(A_log)
        y = _selective_scan(x_b, delta, a, b, c)
        y = y + x_b * D_param
        y = y * jax.nn.silu(res)
        return y @ out_proj_w.T + out_proj_b

    def _L1_ffn_ref(x, w_up, w_down):
        import jax, jax.numpy as jnp
        import numpy as np
        EPS = 1e-08

        def _ternary_linear(x, w):
            alpha = jnp.mean(jnp.abs(w))
            w_t = jnp.sign(w) * (jnp.abs(w) > 0.5 * alpha).astype(w.dtype)
            w_q = w + jax.lax.stop_gradient(w_t - w)
            d = x.shape[-1]
            rms = jnp.sqrt(jnp.sum(x * x, axis=-1, keepdims=True)) / jnp.sqrt(jnp.asarray(d, x.dtype))
            x_norm = x / (rms + EPS)
            return jnp.einsum('bsd,fd->bsf', x_norm, w_q)
        h = jax.nn.gelu(_ternary_linear(x, w_up), approximate=False)
        return _ternary_linear(h, w_down)
    x = L0_attn_x
    x = x + 0.5 * _L0_ffn_ref(_layernorm(x, axis=-1), L0_ffn_Wg, L0_ffn_w1, L0_ffn_w2)
    x = x + _L0_attn_ref(_layernorm(x, axis=-1), L0_attn_w_qkv, L0_attn_w_out, L0_attn_b_out)
    x = x + 0.5 * _L0_ffn_ref(_layernorm(x, axis=-1), L0_ffn_Wg, L0_ffn_w1, L0_ffn_w2)
    x = x + 0.5 * _L1_ffn_ref(_layernorm(x, axis=-1), L1_ffn_w_up, L1_ffn_w_down)
    x = x + _L1_attn_ref(_layernorm(x, axis=-1), L1_attn_in_proj_w, L1_attn_in_proj_b, L1_attn_conv_w, L1_attn_conv_b, L1_attn_x_proj_w, L1_attn_dt_proj_w, L1_attn_dt_proj_b, L1_attn_A_log, L1_attn_D_param, L1_attn_out_proj_w, L1_attn_out_proj_b)
    x = x + 0.5 * _L1_ffn_ref(_layernorm(x, axis=-1), L1_ffn_w_up, L1_ffn_w_down)
    return x

_drawn_inputs = setup_inputs


def setup_inputs(seed=0):
    import zlib

    import numpy as np

    out = dict(_drawn_inputs(seed))
    spreads = {'L1_attn_in_proj_b': (0.0, 0.8),
     'L1_attn_conv_b': (0.0, 0.8),
     'L1_attn_dt_proj_b': (0.0, 0.8),
     'L1_attn_D_param': (1.0, 0.6),
     'L1_attn_out_proj_b': (0.0, 0.8)}
    factors = {'L0_ffn_Wg': 8.0,
     'L1_attn_in_proj_w': 8.0,
     'L1_attn_conv_w': 8.0,
     'L1_attn_x_proj_w': 8.0,
     'L1_attn_dt_proj_w': 8.0,
     'L1_attn_A_log': 8.0,
     'L1_attn_out_proj_w': 8.0}
    for name, (base, spread) in spreads.items():
        noise = np.random.default_rng([zlib.crc32(name.encode()), seed]).standard_normal(out[name].shape)
        drawn = base * np.exp(spread * noise) if base else spread * noise
        out[name] = jnp.asarray(drawn.astype(out[name].dtype))
    for name, factor in factors.items():
        out[name] = (out[name] * factor).astype(out[name].dtype)
    return out
```

```python
from contextlib import ExitStack

import concourse.bass as bass
from concourse import mybir

F32 = mybir.dt.float32
BF16 = mybir.dt.bfloat16
ALU = mybir.AluOpType
ACT = mybir.ActivationFunctionType
AX = mybir.AxisListType

P = 128
CH = 512
TPC = CH // P
LN_EPS = 1e-5
RMS_EPS = 1e-8
F32_EPS = 1.1920928955078125e-07
MASKED = -1.0e30
FREE = 1


def macaron_kernel(nc, x_in, w_qkvT, w_outT, b_out, Wg, w1, w2, in_wT, in_b, conv_w, conv_b,
                   xp_wT, dt_wT, dt_b, A_log, D_param, op_wT, op_b, upT, downT, out):
    B, L, D = x_in.shape
    T = B * L
    NT = T // P
    NC = T // CH
    TPB = L // P
    E = Wg.shape[1]
    DFF = w1.shape[1]
    KB = DFF // P
    H, HD, WIN = 16, 8, 64
    JG = 4
    HPG = H // JG
    DI = in_wT.shape[1] // 2
    HV = DI // P
    DC = conv_w.shape[1]
    NS = A_log.shape[1]
    RK = dt_wT.shape[0]
    KS3 = 3 * 2 * NS

    x_src = x_in.rearrange("b (t p) d -> p (b t) d", p=P)
    x_dst = out.rearrange("b (t p) d -> p (b t) d", p=P)

    with ExitStack() as ctx:
        def sb(name, shape, dt=F32):
            return ctx.enter_context(nc.sbuf_tensor(name, shape, dt))

        def sem(name):
            return ctx.enter_context(nc.semaphore(name))

        x = sb("x", [P, NT * D])
        wqkv = sb("wqkv", [P, 3 * P])
        wo = sb("wo", [P, P])
        bo = sb("bo", [1, P])
        wg = sb("wg", [P, E])
        w1s = sb("w1s", [P, DFF])
        w2s = sb("w2s", [P, KB, P])
        wup = sb("wup", [P, DFF])
        wdn = sb("wdn", [P, KB, P])
        win = sb("win", [P, 2 * DI])
        bin_ = sb("bin_", [P, 2 * HV])
        cw = sb("cw", [P, HV, DC])
        cb = sb("cb", [P, HV])
        wx = sb("wx", [P, HV, KS3 + RK])
        wdt = sb("wdt", [P, DI])
        bdt = sb("bdt", [P, HV])
        alog = sb("alog", [P, HV * NS])
        aneg = sb("aneg", [P, HV * NS])
        dpar = sb("dpar", [P, HV])
        wop = sb("wop", [P, HV, P])
        bop = sb("bop", [1, P])
        ident = sb("ident", [P, P])
        identb = sb("identb", [P, P], BF16)
        ones = sb("ones", [P, P])
        mask = sb("mask", [P, NT, P], BF16)
        qmask = sb("qmask", [P, HPG])
        sel = sb("sel", [KS3, 2 * NS, P], BF16)
        diagD = sb("diagD", [P, HV, P])
        mhalf = sb("mhalf", [P, H])
        half = sb("half", [P, H])
        mone = sb("mone", [P, H])
        lneps = sb("lneps", [P, TPC])
        rmseps = sb("rmseps", [P, TPC])
        carrier = sb("carrier", [P, 2])
        stats = sb("stats", [P, TPC, 6])
        mv = sb("mv", [P, TPC, 2])
        veps = sb("veps", [P, TPC])
        rstd = sb("rstd", [P, TPC])
        sd = sb("sd", [P, TPC])
        rr = sb("rr", [P, TPC])
        nscale = sb("nscale", [P, TPC])
        xn = sb("xn", [P, CH])
        xT = sb("xT", [P, CH])
        hT = sb("hT", [P, KB, CH])
        hsq = sb("hsq", [P, KB, CH])
        top = sb("top", [P, TPC, 8])
        topd = sb("topd", [P, TPC, 8])
        tope = sb("tope", [P, TPC, 8])
        gz = sb("gz", [P, 8, TPC])
        g12 = sb("g12", [P, TPC, 2])
        gn = sb("gn", [P, TPC, 2])
        gs = sb("gs", [P, TPC])
        aw = sb("aw", [P, DFF])
        asum = sb("asum", [P, 2])
        thr = sb("thr", [P, 4])
        xw = sb("xw", [P, P // 2 + P])
        qm = sb("qm", [P, HPG, P])
        kT = sb("kT", [P, P // 2 + P])
        va = sb("va", [P, 2, H, HD + 1])
        ssub = sb("ssub", [P, JG, HPG * P])
        pT = sb("pT", [P, 2, HPG * P])
        smax = sb("smax", [P, H])
        rden = sb("rden", [P, H])
        cx = sb("cx", [P, H, HD])
        cxT = sb("cxT", [P, P])
        xb = sb("xb", [P, 2, HV, DC - 1 + CH])
        cacc = sb("cacc", [P, HV, CH])
        u = sb("u", [P, HV, T])
        g = sb("g", [P, HV, T])
        s3 = sb("s3", [KS3, L], BF16)
        hi3 = sb("hi3", [KS3, L], BF16)
        r3 = sb("r3", [KS3, L])
        xd = sb("xd", [P, L])
        delta = sb("delta", [P, HV, L])
        ea = sb("ea", [P, HV, L])
        eb = sb("eb", [P, HV, L])
        du = sb("du", [P, HV, L])
        dA = sb("dA", [P, HV, L])
        dBu = sb("dBu", [P, HV, L])
        hst = sb("hst", [P, HV, L])
        hC = sb("hC", [P, HV, L])
        Cs = sb("Cs", [P, L])

        bank = [ctx.enter_context(nc.psum_tensor(f"bank{i}", [P, 512], F32)) for i in range(4)]
        bk45 = ctx.enter_context(nc.psum_tensor("bk45", [P, 1024], F32))
        bk67 = ctx.enter_context(nc.psum_tensor("bk67", [P, 1024], F32))
        psT, psD = bk45[:, 0:512], bk45[:, 512:1024]
        psG, psQ = bk67[:, 0:512], bk67[:, 512:1024]

        w_in = sem("w_in")
        x_inp = sem("x_inp")
        set_pool = sem("set_pool")
        set_pool_step = sem("set_pool_step")
        set_pe = sem("set_pe")
        set_act = sem("set_act")
        set_dve = sem("set_dve")
        set_dve_step = sem("set_dve_step")
        out_done = sem("out_done")

        class Ffn:

            def __init__(self, name, ternary, w_up, w_down, func):
                self.ternary, self.w_up, self.w_down, self.func = ternary, w_up, w_down, func
                self.stats = sem(name + "_stats")
                self.ln_step = sem(name + "_lnstep")
                self.rstd_step = sem(name + "_rstep")
                self.rstd = sem(name + "_rstd")
                self.xn = sem(name + "_xn")
                self.xpose = sem(name + "_xpose")
                self.xT = sem(name + "_xT")
                self.up = sem(name + "_up")
                self.h = sem(name + "_h")
                self.logit = sem(name + "_logit")
                self.gstep = sem(name + "_gstep")
                self.topd = sem(name + "_topd")
                self.tope = sem(name + "_tope")
                self.gsum = sem(name + "_gsum")
                self.gpstep = sem(name + "_gpstep")
                self.scale = sem(name + "_scale")
                self.hsq = sem(name + "_hsq")
                self.ssq = sem(name + "_ssq")
                self.down = sem(name + "_down")
                self.xupd = sem(name + "_xupd")

        moe0 = Ffn("moe0", False, w1s, w2s, ACT.Relu)
        moe1 = Ffn("moe1", False, w1s, w2s, ACT.Relu)
        ter0 = Ffn("ter0", True, wup, wdn, ACT.Gelu)
        ter1 = Ffn("ter1", True, wup, wdn, ACT.Gelu)

        at = {k: sem("at_" + k) for k in (
            "stats", "ln_step", "rstd_step", "rstd", "xn", "xpose", "xw", "xsh", "qkv", "qk", "v", "s", "max", "sub",
            "p", "pt", "pts", "pvg", "pv", "rden", "cx", "cxt", "cxs", "op", "xupd", "ksh")}
        m1 = {k: sem("m1_" + k) for k in (
            "stats", "ln_step", "rstd_step", "rstd", "xn", "xpose", "xT", "proj", "xb", "carry", "cstep", "conv", "u", "g")}
        m2 = {k: sem("m2_" + k) for k in (
            "xp", "s3step", "r3", "xd", "dt", "ea", "eb", "ln", "poolstep", "corr", "dstep", "delta",
            "B", "C", "Cs", "mul", "yg", "op", "xupd")}
        dA_done = [sem(f"dA_done{h}") for h in range(HV)]
        scanned = [sem(f"scanned{h}") for h in range(HV)]
        hC_done = [sem(f"hC_done{h}") for h in range(HV)]
        reduced = [sem(f"reduced{h}") for h in range(HV)]

        def xs(tok0, n):
            return x[:, bass.ds(tok0, n)]

        def carry_wait_vector():
            nc.vector.tensor_copy(carrier[:, 0:1], half[:, 0:1])

        def carry_wait_pool():
            nc.gpsimd.tensor_tensor(carrier[:, 1:2], half[:, 0:1], half[:, 0:1], ALU.mult)

        def stepper(eng, s, base):
            count = [0]

            def link(ins):
                count[0] += 1
                ins.then_inc(s, 1)
                eng.wait_ge(s, base + count[0])
            return link

        LN_DVE = 1
        LN_POOL = {False: 1, True: 6}

        def ln_vector(dve, stats_s, step_s, rstd_s, xn_s, xpose_s, idx, tok0, nt, scale):
            link = stepper(dve, step_s, idx * LN_DVE)
            for i in range(nt):
                last = nc.vector.bn_stats(stats[:, i, :], xs(tok0 + i * D, D))
            link(last)
            carry_wait_vector()
            for i in range(nt):
                last = nc.vector.bn_aggr(mv[:, i, :], stats[:, i, :])
            last.then_inc(stats_s, 1)
            dve.wait_ge(step_s, idx * LN_DVE + 1)
            dve.wait_ge(rstd_s, idx + 1)
            if not isinstance(idx, int) or idx > 0:
                dve.wait_ge(xpose_s, idx)
            for i in range(nt):
                last = nc.vector.tensor_scalar(xn[:, i * D:(i + 1) * D], xs(tok0 + i * D, D), mv[:, i, 0:1],
                                               scale[:, i:i + 1], ALU.subtract, ALU.mult)
            last.then_inc(xn_s, 1)

        def ln_pool(pool, stats_s, step_s, rstd_s, idx, nt, ternary):
            link = stepper(pool, step_s, idx * LN_POOL[ternary])
            pool.wait_ge(stats_s, idx + 1)
            link(nc.gpsimd.tensor_tensor(veps[:, 0:nt], mv[:, 0:nt, 1], lneps[:, 0:nt], ALU.add))
            if not ternary:
                nc.gpsimd.tensor_tensor(rstd[:, 0:nt], veps[:, 0:nt], mhalf[:, 0:nt], ALU.pow).then_inc(rstd_s, 1)
                return
            link(nc.gpsimd.tensor_tensor(rstd[:, 0:nt], veps[:, 0:nt], mhalf[:, 0:nt], ALU.pow))
            link(nc.gpsimd.tensor_tensor(sd[:, 0:nt], mv[:, 0:nt, 1], half[:, 0:nt], ALU.pow))
            link(nc.gpsimd.tensor_tensor(rr[:, 0:nt], sd[:, 0:nt], rstd[:, 0:nt], ALU.mult))
            link(nc.gpsimd.tensor_tensor(veps[:, 0:nt], rr[:, 0:nt], rmseps[:, 0:nt], ALU.add))
            link(nc.gpsimd.tensor_tensor(rr[:, 0:nt], veps[:, 0:nt], mone[:, 0:nt], ALU.pow))
            nc.gpsimd.tensor_tensor(nscale[:, 0:nt], rstd[:, 0:nt], rr[:, 0:nt], ALU.mult).then_inc(rstd_s, 1)

        def ffn_vector(dve, f, before, count):
            dve.wait_ge(before, count)
            scale = nscale if f.ternary else rstd

            def ln(c):
                ln_vector(dve, f.stats, f.ln_step, f.rstd, f.xn, f.xpose, c, c * CH, TPC, scale)

            def gate(c):
                link = stepper(dve, f.gstep, c)
                dve.wait_ge(f.logit, c + 1)
                carry_wait_vector()
                for i in range(TPC):
                    last = nc.vector.max(top[:, i, :], psG[:, i * 8:(i + 1) * 8])
                link(last)
                nc.vector.tensor_tensor(topd[:, :, :], top[:, :, :], top[:, :, 0:1].to_broadcast([P, TPC, 8]),
                                        ALU.subtract).then_inc(f.topd, 1)
                dve.wait_ge(f.tope, c + 1)
                nc.vector.tensor_reduce(gz[:, 0, :], tope[:, :, :], AX.X, ALU.add).then_inc(f.gsum, 1)

            def rms(c):
                dve.wait_ge(f.ssq, c + 1 + FREE)
                nc.vector.tensor_scalar(gz[:, 0, :], psG[:, 0:TPC], 1.0 / DFF, None, ALU.mult).then_inc(f.gsum, 1)

            def update(c):
                dve.wait_ge(f.down, c + 1)
                dve.wait_ge(f.scale, c + 1)
                for i in range(TPC):
                    at_ = c * CH + i * D
                    last = nc.vector.scalar_tensor_tensor(out=xs(at_, D), in0=psD[:, i * D:(i + 1) * D],
                                                          scalar=gs[:, i:i + 1], in1=xs(at_, D),
                                                          op0=ALU.mult, op1=ALU.add)
                last.then_inc(f.xupd, 1)

            side = rms if f.ternary else gate
            ln(0)
            with dve.Fori(0, NC - 1) as c:
                ln(c + 1)
                side(c)
                update(c)
            side(NC - 1)
            update(NC - 1)

        def ffn_pool(pool, f):
            def ln(c):
                ln_pool(pool, f.stats, f.rstd_step, f.rstd, c, TPC, f.ternary)

            def gate(c):
                link = stepper(pool, f.gpstep, c * 9)
                pool.wait_ge(f.gsum, c + 1)
                link(nc.gpsimd.tensor_tensor(gz[:, 1, :], gz[:, 0, :], mone[:, 0:TPC], ALU.pow))
                link(nc.gpsimd.tensor_tensor(g12[:, :, 0], tope[:, :, 0], gz[:, 1, :], ALU.mult))
                link(nc.gpsimd.tensor_tensor(g12[:, :, 1], tope[:, :, 1], gz[:, 1, :], ALU.mult))
                link(nc.gpsimd.tensor_tensor(gz[:, 2, :], g12[:, :, 0], g12[:, :, 1], ALU.add))
                carry_wait_pool()
                link(nc.gpsimd.tensor_scalar(gz[:, 3, :], gz[:, 2, :], F32_EPS, None, ALU.max))
                link(nc.gpsimd.tensor_tensor(gz[:, 4, :], gz[:, 3, :], mone[:, 0:TPC], ALU.pow))
                link(nc.gpsimd.tensor_tensor(gn[:, :, 0], g12[:, :, 0], gz[:, 4, :], ALU.mult))
                link(nc.gpsimd.tensor_tensor(gn[:, :, 1], g12[:, :, 1], gz[:, 4, :], ALU.mult))
                if not isinstance(c, int) or c > 0:
                    pool.wait_ge(f.xupd, c + FREE)
                link(nc.gpsimd.tensor_tensor(gz[:, 5, :], gn[:, :, 0], gn[:, :, 1], ALU.add))
                nc.gpsimd.tensor_tensor(gs[:, :], gz[:, 5, :], half[:, 0:TPC], ALU.mult).then_inc(f.scale, 1)

            def squares(c):
                for k in range(KB):
                    pool.wait_ge(f.h, c * KB + k + 1)
                    if not isinstance(c, int) or c > 0:
                        pool.wait_ge(f.ssq, c + FREE)
                    nc.gpsimd.tensor_tensor(hsq[:, k, :], hT[:, k, :], hT[:, k, :], ALU.mult).then_inc(f.hsq, 1)

            def rms(c):
                link = stepper(pool, f.gpstep, c * 3)
                pool.wait_ge(f.gsum, c + 1)
                link(nc.gpsimd.tensor_tensor(gz[:, 1, :], gz[:, 0, :], half[:, 0:TPC], ALU.pow))
                link(nc.gpsimd.tensor_tensor(gz[:, 2, :], gz[:, 1, :], rmseps[:, 0:TPC], ALU.add))
                if not isinstance(c, int) or c > 0:
                    pool.wait_ge(f.xupd, c + FREE)
                link(nc.gpsimd.tensor_tensor(gz[:, 3, :], gz[:, 2, :], mone[:, 0:TPC], ALU.pow))
                nc.gpsimd.tensor_tensor(gs[:, :], gz[:, 3, :], half[:, 0:TPC], ALU.mult).then_inc(f.scale, 1)

            ln(0)
            with pool.Fori(0, NC - 1) as c:
                ln(c + 1)
                if f.ternary:
                    squares(c)
                    rms(c)
                else:
                    gate(c)
            if f.ternary:
                squares(NC - 1)
                rms(NC - 1)
            else:
                gate(NC - 1)

        def transposes(pe, xn_s, xpose_s, xT_s, idx):
            pe.wait_ge(xn_s, idx + 1)
            if not isinstance(idx, int) or idx > 0:
                pe.wait_ge(xT_s, idx)
            for i in range(TPC):
                last = nc.tensor.transpose(psT[:, i * P:(i + 1) * P], xn[:, i * P:(i + 1) * P], ident[:, :])
            last.then_inc(xpose_s, 1)

        def ffn_tensor(pe, f):
            def up(c):
                pe.wait_ge(f.xT, c + 1)
                if not f.ternary:
                    if not isinstance(c, int) or c > 0:
                        pe.wait_ge(f.topd, c + FREE)
                    for i in range(TPC):
                        last = nc.tensor.matmul(psG[:, i * 8:(i + 1) * 8], xT[:, i * P:(i + 1) * P], wg[:, :],
                                                start=True, stop=True)
                    last.then_inc(f.logit, 1)
                for k in range(KB):
                    nc.tensor.matmul(bank[k][:, :], f.w_up[:, k * P:(k + 1) * P], xT[:, :],
                                     start=True, stop=True).then_inc(f.up, 1)

            def down(c):
                if not isinstance(c, int) or c > 0:
                    pe.wait_ge(f.xupd, c + FREE)
                for k in range(KB):
                    pe.wait_ge(f.h, c * KB + k + 1)
                    for i in range(TPC):
                        last = nc.tensor.matmul(psD[:, i * P:(i + 1) * P], hT[:, k, i * P:(i + 1) * P],
                                                f.w_down[:, k, :], start=(k == 0 and i == 0), stop=(k == KB - 1),
                                                skip_group_check=True)
                last.then_inc(f.down, 1)
                if f.ternary:
                    for k in range(KB):
                        pe.wait_ge(f.hsq, c * KB + k + 1)
                        for i in range(TPC):
                            last = nc.tensor.matmul(psG[:, i:i + 1], hsq[:, k, i * P:(i + 1) * P], ones[:, 0:1],
                                                    start=(k == 0 and i == 0), stop=(k == KB - 1),
                                                    skip_group_check=True)
                    last.then_inc(f.ssq, 1)

            transposes(pe, f.xn, f.xpose, f.xT, 0)
            with pe.Fori(0, NC - 1) as c:
                up(c)
                transposes(pe, f.xn, f.xpose, f.xT, c + 1)
                down(c)
            up(NC - 1)
            down(NC - 1)

        def copy_xT(act, xpose_s, xT_s, used_s, used, idx):
            act.wait_ge(xpose_s, idx + 1)
            if not isinstance(idx, int) or idx > 0:
                act.wait_ge(used_s, used)
            nc.scalar.copy(xT[:, :], psT).then_inc(xT_s, 1)

        def ffn_scalar(act, f):
            def hidden(c):
                for k in range(KB):
                    act.wait_ge(f.up, c * KB + k + 1)
                    nc.scalar.activation(hT[:, k, :], bank[k][:, :], f.func).then_inc(f.h, 1)

            def gate(c):
                act.wait_ge(f.topd, c + 1 + FREE)
                nc.scalar.activation(tope[:, :, :], topd[:, :, :], ACT.Exp).then_inc(f.tope, 1)

            copy_xT(act, f.xpose, f.xT, f.up, 0, 0)
            with act.Fori(0, NC - 1) as c:
                hidden(c)
                copy_xT(act, f.xpose, f.xT, f.up, (c + 1) * KB, c + 1)
                if not f.ternary:
                    gate(c)
            hidden(NC - 1)
            if not f.ternary:
                gate(NC - 1)

        def over_tiles(eng, body):
            body(0, True, False)
            with eng.Fori(1, NT - 1) as t:
                body(t, False, False)
            body(NT - 1, False, True)

        def attn_vector(dve):
            dve.wait_ge(moe0.xupd, NC + FREE)
            psO = psD[:, 0:H * (HD + 1)].rearrange("p (h e) -> p h e", e=HD + 1)
            psP = psD[:, 160:160 + P]

            def ln(t):
                ln_vector(dve, at["stats"], at["ln_step"], at["rstd"], at["xn"], at["xpose"], t, t * D, 1, rstd)

            def context(t):
                dve.wait_ge(at["pv"], t + 1)
                nc.vector.reciprocal(rden[:, :], psO[:, :, HD]).then_inc(at["rden"], 1)
                dve.wait_ge(at["rden"], t + 1)
                nc.vector.tensor_tensor(cx[:, :, :], psO[:, :, 0:HD],
                                        rden[:, :].rearrange("p (h o) -> p h o", o=1).to_broadcast([P, H, HD]),
                                        ALU.mult).then_inc(at["cx"], 1)

            def soften(t, j):
                s3d = bank[j][:, :].rearrange("p (a k) -> p a k", a=HPG)
                dve.wait_ge(at["s"], t * JG + j + 1)
                nc.vector.tensor_reduce(smax[:, j * HPG:(j + 1) * HPG], s3d, AX.X, ALU.max).then_inc(at["max"], 1)
                dve.wait_ge(at["max"], t * JG + j + 1)
                m = smax[:, j * HPG:(j + 1) * HPG].rearrange("p (a o) -> p a o", o=1).to_broadcast([P, HPG, P])
                if not isinstance(t, int) or t > 0:
                    dve.wait_ge(at["pt"], t * JG - JG + j + 1)
                nc.vector.tensor_tensor(ssub[:, j, :].rearrange("p (a k) -> p a k", a=HPG), s3d, m,
                                        ALU.subtract).then_inc(at["sub"], 1)

            def update(t):
                dve.wait_ge(at["op"], t + 1)
                nc.vector.tensor_tensor(xs(t * D, D), psP, xs(t * D, D), ALU.add).then_inc(at["xupd"], 1)

            def body(t, first, last):
                if not first:
                    context(t - 1)
                if not last:
                    ln(t + 1)
                soften(t, 0)
                if not first:
                    update(t - 1)
                for j in range(1, JG):
                    soften(t, j)

            ln(0)
            over_tiles(dve, body)
            context(NT - 1)
            update(NT - 1)

        def attn_pool(pool):
            ln_pool(pool, at["stats"], at["rstd_step"], at["rstd"], 0, 1, False)
            with pool.Fori(1, NT) as t:
                ln_pool(pool, at["stats"], at["rstd_step"], at["rstd"], t, 1, False)

        def attn_tensor(pe):
            psO = psD[:, 0:H * (HD + 1)].rearrange("p (h e) -> p h e", e=HD + 1)
            psP = psD[:, 160:160 + P]
            psX = psD[:, 288:288 + P]
            psPT = [psT, psG]

            def xpose(t):
                pe.wait_ge(at["xn"], t + 1)
                if not isinstance(t, int) or t > 1:
                    pe.wait_ge(at["xupd"], t - 1)
                nc.tensor.transpose(psX, xn[:, 0:P], ident[:, :]).then_inc(at["xpose"], 1)

            def qkv(t):
                pe.wait_ge(at["xw"], t + 1)
                if not isinstance(t, int) or t > 0:
                    pe.wait_ge(at["qk"], t)
                    pe.wait_ge(at["v"], t)
                for n in range(2):
                    nc.tensor.matmul(psQ[:, n * P:(n + 1) * P], wqkv[:, n * P:(n + 1) * P], xw[:, 64:64 + P],
                                     start=True, stop=True)
                for s in range(2):
                    last = nc.tensor.matmul(psQ[:, (2 + s) * P:(3 + s) * P], xw[:, 64 * s:64 * s + P],
                                            wqkv[:, 2 * P:3 * P], start=True, stop=True)
                last.then_inc(at["qkv"], 1)

            def scores(t, j):
                if j == 0:
                    pe.wait_ge(at["qk"], t + 1)
                if not isinstance(t, int) or t > 0:
                    pe.wait_ge(at["sub"], t * JG - JG + j + 1)
                for a in range(HPG):
                    nc.tensor.matmul(bank[j][:, a * P:(a + 1) * P], identb[:, :], mask[:, t, :],
                                     start=(a == 0), stop=False, skip_group_check=True)
                for a in range(HPG):
                    for s in range(2):
                        last = nc.tensor.matmul(bank[j][64 * s:64 * s + 64, a * P:(a + 1) * P],
                                                qm[32 * j:32 * j + 32, a, 64 * s:64 * s + 64],
                                                kT[32 * j:32 * j + 32, 64 * s:64 * s + P],
                                                start=False, stop=True, skip_group_check=True)
                last.then_inc(at["s"], 1)

            def prob_t(t, j):
                pe.wait_ge(at["p"], t * JG + j + 1)
                if j >= 2:
                    pe.wait_ge(at["pts"], t * JG + j - 1)
                elif not isinstance(t, int) or t > 0:
                    pe.wait_ge(at["pts"], t * JG + j - 1)
                for a in range(HPG):
                    last = nc.tensor.transpose(psPT[j % 2][:, a * P:(a + 1) * P], ssub[:, j, a * P:(a + 1) * P],
                                               ident[:, :])
                last.then_inc(at["pt"], 1)

            def values(t, j):
                pe.wait_ge(at["pts"], t * JG + j + 1)
                if j == 0:
                    pe.wait_ge(at["v"], t + 1)
                    if not isinstance(t, int) or t > 0:
                        pe.wait_ge(at["xupd"], t)
                for a in range(HPG):
                    h = j * HPG + a
                    for s in range(2):
                        last = nc.tensor.matmul(psO[64 * s:64 * s + 64, h, :],
                                                pT[:, j % 2, a * P + 64 * s:a * P + 64 * s + 64],
                                                va[:, s, h, :], start=True, stop=True)
                if j == JG - 1:
                    last.then_inc(at["pv"], 1)
                else:
                    last.then_inc(at["pvg"], 1)

            def body(t, first, last):
                scores(t, 0)
                if not first:
                    ctx_t(t - 1)
                scores(t, 1)
                if not first:
                    project(t - 1)
                scores(t, 2)
                if not last:
                    xpose(t + 1)
                scores(t, 3)
                if not last:
                    qkv(t + 1)
                prob_t(t, 0)
                prob_t(t, 1)
                values(t, 0)
                prob_t(t, 2)
                values(t, 1)
                prob_t(t, 3)
                values(t, 2)
                values(t, 3)

            def ctx_t(t):
                pe.wait_ge(at["cx"], t + 1)
                nc.tensor.transpose(psX, cx[:, :, :].rearrange("p h e -> p (h e)"), ident[:, :]).then_inc(at["cxt"], 1)

            def project(t):
                pe.wait_ge(at["cxs"], t + 1)
                nc.tensor.matmul(psP, cxT[:, :], wo[:, :], start=True, stop=False)
                nc.tensor.matmul(psP, ones[0:1, :], bo[0:1, :], start=False, stop=True).then_inc(at["op"], 1)

            xpose(0)
            qkv(0)
            over_tiles(pe, body)
            ctx_t(NT - 1)
            project(NT - 1)

        def attn_scalar(act):
            psX = psD[:, 288:288 + P]
            psPT = [psT, psG]

            def copy_x(t):
                if not isinstance(t, int) or t > 0:
                    act.wait_ge(at["qkv"], t)
                    nc.scalar.copy(xw[:, 0:64], xw[:, P:P + 64]).then_inc(at["xsh"], 1)
                    act.wait_ge(at["xsh"], t)
                act.wait_ge(at["xpose"], t + 1)
                nc.scalar.copy(xw[:, 64:64 + P], psX).then_inc(at["xw"], 1)

            def copy_qk(t):
                act.wait_ge(at["qkv"], t + 1)
                if not isinstance(t, int) or t > 0:
                    act.wait_ge(at["s"], t * JG)
                    nc.scalar.copy(kT[:, 0:64], kT[:, P:P + 64]).then_inc(at["ksh"], 1)
                for a in range(HPG):
                    nc.scalar.activation(qm[:, a, :], psQ[:, 0:P], ACT.Copy, scale=qmask[:, a:a + 1])
                if not isinstance(t, int) or t > 0:
                    act.wait_ge(at["ksh"], t)
                nc.scalar.copy(kT[:, 64:64 + P], psQ[:, P:2 * P]).then_inc(at["qk"], 1)

            def copy_v(t):
                act.wait_ge(at["qkv"], t + 1)
                if not isinstance(t, int) or t > 0:
                    act.wait_ge(at["pv"], t)
                nc.scalar.copy(va[:, :, :, 0:HD], psQ[:, 2 * P:4 * P].rearrange("p (s h e) -> p s h e", s=2, e=HD)
                               ).then_inc(at["v"], 1)

            def probs(t, j):
                act.wait_ge(at["sub"], t * JG + j + 1)
                nc.scalar.activation(ssub[:, j, :], ssub[:, j, :], ACT.Exp).then_inc(at["p"], 1)

            def probs_t(t, j):
                act.wait_ge(at["pt"], t * JG + j + 1)
                if j >= 2:
                    act.wait_ge(at["pvg"], t * (JG - 1) + j - 1)
                elif not isinstance(t, int) or t > 0:
                    act.wait_ge(at["pv"], t)
                nc.scalar.copy(pT[:, j % 2, :], psPT[j % 2]).then_inc(at["pts"], 1)

            def body(t, first, last):
                copy_v(t)
                if not first:
                    copy_ctx(t - 1)
                probs(t, 0)
                if not last:
                    copy_x(t + 1)
                for j in range(1, JG):
                    probs(t, j)
                probs_t(t, 0)
                probs_t(t, 1)
                if not last:
                    copy_qk(t + 1)
                probs_t(t, 2)
                probs_t(t, 3)

            def copy_ctx(t):
                act.wait_ge(at["cxt"], t + 1)
                nc.scalar.copy(cxT[:, :], psX).then_inc(at["cxs"], 1)

            copy_x(0)
            copy_qk(0)
            over_tiles(act, body)
            copy_ctx(NT - 1)

        
        CPB = L // CH
        PROJ = 2 * HV

        def ssm1_vector(dve):
            dve.wait_ge(ter0.xupd, NC + FREE)

            def ln(c):
                ln_vector(dve, m1["stats"], m1["ln_step"], m1["rstd"], m1["xn"], m1["xpose"], c, c * CH, TPC, rstd)

            def conv(c, r):
                link = stepper(dve, m1["cstep"], c * (DC - 1))
                dve.wait_ge(m1["xb"], (c + 1) * HV + FREE)
                if not isinstance(c, int) or c > 0:
                    dve.wait_ge(m1["u"], c + FREE)
                for k in range(DC):
                    for h in range(HV):
                        src = xb[:, r, h, k:k + CH]
                        if k == 0:
                            last = nc.vector.tensor_scalar(cacc[:, h, :], src, cw[:, h, k:k + 1], cb[:, h:h + 1],
                                                           ALU.mult, ALU.add)
                        else:
                            last = nc.vector.scalar_tensor_tensor(out=cacc[:, h, :], in0=src, scalar=cw[:, h, k:k + 1],
                                                                  in1=cacc[:, h, :], op0=ALU.mult, op1=ALU.add)
                    if k < DC - 1:
                        link(last)
                last.then_inc(m1["conv"], 1)

            ln(0)
            with dve.Fori(0, B - 1) as b:
                for r in range(CPB):
                    ln(b * CPB + r + 1)
                    conv(b * CPB + r, r)
            c0 = (B - 1) * CPB
            for r in range(CPB):
                if r < CPB - 1:
                    ln(c0 + r + 1)
                conv(c0 + r, r)

        def ssm1_pool(pool):
            with pool.Fori(0, NC) as c:
                ln_pool(pool, m1["stats"], m1["rstd_step"], m1["rstd"], c, TPC, False)

        def ssm1_tensor(pe):
            def proj(c):
                pe.wait_ge(m1["xT"], c + 1)
                if not isinstance(c, int) or c > 0:
                    pe.wait_ge(m1["xb"], c * HV + FREE)
                    pe.wait_ge(m1["g"], c + FREE)
                for k in range(PROJ):
                    nc.tensor.matmul(bank[k][:, :], win[:, k * P:(k + 1) * P], xT[:, :],
                                     start=True, stop=True).then_inc(m1["proj"], 1)

            transposes(pe, m1["xn"], m1["xpose"], m1["xT"], 0)
            with pe.Fori(0, NC - 1) as c:
                proj(c)
                transposes(pe, m1["xn"], m1["xpose"], m1["xT"], c + 1)
            proj(NC - 1)

        def ssm1_scalar(act):
            def chunk(c, r, last):
                if r > 0:
                    act.wait_ge(m1["xb"], c * HV + FREE)
                    for h in range(HV):
                        i = nc.scalar.copy(xb[:, r, h, 0:DC - 1], xb[:, r - 1, h, CH:CH + DC - 1])
                for h in range(HV):
                    act.wait_ge(m1["proj"], c * PROJ + h + 1)
                    nc.scalar.activation(xb[:, r, h, DC - 1:], bank[h][:, :], ACT.Identity,
                                         bias=bin_[:, h:h + 1]).then_inc(m1["xb"], 1)
                act.wait_ge(m1["proj"], (c + 1) * PROJ)
                for h in range(HV):
                    i = nc.scalar.activation(g[:, h, bass.ds(c * CH, CH)], bank[HV + h][:, :], ACT.Silu,
                                             bias=bin_[:, HV + h:HV + h + 1])
                i.then_inc(m1["g"], 1)
                if not last:
                    copy_xT(act, m1["xpose"], m1["xT"], m1["proj"], (c + 1) * PROJ, c + 1)
                act.wait_ge(m1["conv"], c + 1)
                for h in range(HV):
                    i = nc.scalar.activation(u[:, h, bass.ds(c * CH, CH)], cacc[:, h, :], ACT.Silu)
                i.then_inc(m1["u"], 1)

            copy_xT(act, m1["xpose"], m1["xT"], m1["proj"], 0, 0)
            with act.Fori(0, B - 1) as b:
                for r in range(CPB):
                    chunk(b * CPB + r, r, False)
            for r in range(CPB):
                chunk((B - 1) * CPB + r, r, r == CPB - 1)

        def ssm2_vector(dve):
            with dve.Fori(0, B) as b:
                link = stepper(dve, m2["s3step"], b * 3)
                dve.wait_ge(m2["xd"], b + 1)
                link(nc.vector.tensor_tensor(r3[:, :], bk45[0:KS3, :], hi3[:, :], ALU.subtract))
                nc.vector.tensor_copy(s3[2 * NS:4 * NS, :], r3[2 * NS:4 * NS, :])
                link(nc.vector.tensor_copy(hi3[4 * NS:KS3, :], r3[4 * NS:KS3, :]))
                link(nc.vector.tensor_tensor(s3[4 * NS:KS3, :], r3[4 * NS:KS3, :], hi3[4 * NS:KS3, :], ALU.subtract))
                nc.vector.tensor_copy(s3[0:2 * NS, :], hi3[0:2 * NS, :]).then_inc(m2["r3"], 1)
                link = stepper(dve, m2["dstep"], b * 3)
                dve.wait_ge(m2["ea"], b + 1)
                for h in range(HV):
                    for r in range(CPB):
                        last = nc.vector.tensor_scalar(delta[:, h, r * CH:(r + 1) * CH], bank[h * CPB + r][:, :],
                                                       bdt[:, h:h + 1], 0.0, ALU.add, ALU.max)
                link(last)
                dve.wait_ge(m2["ln"], b + 1)
                link(nc.vector.tensor_tensor(delta[:, :, :], delta[:, :, :], du[:, :, :], ALU.add))
                dve.wait_ge(m2["corr"], b + 1)
                link(nc.vector.tensor_tensor(delta[:, :, :], delta[:, :, :], eb[:, :, :], ALU.add))
                nc.vector.tensor_tensor(du[:, :, :], delta[:, :, :], u[:, :, bass.ds(b * L, L)],
                                        ALU.mult).then_inc(m2["delta"], 1)
                dve.wait_ge(m2["delta"], b + 1)
                carry_wait_vector()
                with dve.Fori(0, NS) as n:
                    k = b * NS + n
                    dve.wait_ge(m2["B"], k + 1)
                    for h in range(HV):
                        nc.vector.tensor_tensor(dBu[:, h, :], bk45[:, :], du[:, h, :], ALU.mult).then_inc(m2["mul"], 1)
                        dve.wait_ge(m2["mul"], k * HV + h + 1 + FREE)
                        dve.wait_ge(dA_done[h], k + 1)
                        dve.wait_ge(hC_done[h], k + FREE)
                        nc.vector.tensor_tensor_scan(hst[:, h, :], dA[:, h, :], dBu[:, h, :], 0.0,
                                                     ALU.mult, ALU.add).then_inc(scanned[h], 1)
                for h in range(HV):
                    dve.wait_ge(reduced[h], (b + 1) * NS + FREE)
                    for r in range(CPB):
                        last = nc.vector.tensor_tensor(hC[:, h, r * CH:(r + 1) * CH], bank[h * CPB + r][:, :],
                                                       g[:, h, bass.ds(b * L + r * CH, CH)], ALU.mult)
                last.then_inc(m2["yg"], 1)
                dve.wait_ge(m2["op"], b + 1)
                nc.vector.tensor_tensor(xs(b * L, L), bk45[:, :], xs(b * L, L), ALU.add).then_inc(m2["xupd"], 1)

        def ssm2_pool(pool):
            with pool.Fori(0, B) as b:
                link = stepper(pool, m2["poolstep"], b)
                pool.wait_ge(m2["eb"], b + 1)
                carry_wait_pool()
                link(nc.gpsimd.tensor_scalar(ea[:, :, :], eb[:, :, :], 1.0, -1.0, ALU.add, ALU.add))
                pool.wait_ge(m2["ln"], b + 1)
                nc.gpsimd.tensor_tensor(eb[:, :, :], eb[:, :, :], ea[:, :, :], ALU.subtract).then_inc(m2["corr"], 1)
                with pool.Fori(0, NS) as n:
                    k = b * NS + n
                    pool.wait_ge(m2["Cs"], k + 1 + FREE)
                    for h in range(HV):
                        pool.wait_ge(scanned[h], k + 1 + FREE)
                        pool.wait_ge(reduced[h], k + FREE)
                        nc.gpsimd.tensor_tensor(hC[:, h, :], hst[:, h, :], Cs[:, :], ALU.mult).then_inc(hC_done[h], 1)

        def ssm2_tensor(pe):
            pe.wait_ge(m1["u"], NC + FREE)
            with pe.Fori(0, B) as b:
                pe.wait_ge(m2["xupd"], b + FREE)
                for r in range(CPB):
                    for h in range(HV):
                        last = nc.tensor.matmul(bk45[0:KS3 + RK, r * CH:(r + 1) * CH], wx[:, h, :],
                                                u[:, h, bass.ds(b * L + r * CH, CH)], start=(h == 0), stop=(h == HV - 1))
                last.then_inc(m2["xp"], 1)
                pe.wait_ge(m2["xd"], b + 1)
                for h in range(HV):
                    for r in range(CPB):
                        last = nc.tensor.matmul(bank[h * CPB + r][:, :], wdt[KS3:KS3 + RK, h * P:(h + 1) * P],
                                                xd[KS3:KS3 + RK, r * CH:(r + 1) * CH], start=True, stop=True)
                last.then_inc(m2["dt"], 1)
                pe.wait_ge(m2["r3"], b + 1)
                pe.wait_ge(m2["delta"], b + 1)
                for h in range(HV):
                    for r in range(CPB):
                        nc.tensor.matmul(bank[h * CPB + r][:, :], diagD[:, h, :], u[:, h, bass.ds(b * L + r * CH, CH)],
                                         start=True, stop=False, skip_group_check=True)

                def spread(n):
                    k = b * NS + n
                    pe.wait_ge(m2["mul"], k * HV + FREE)
                    for r in range(CPB):
                        last = nc.tensor.matmul(bk45[:, r * CH:(r + 1) * CH], sel[:, n, :], s3[:, r * CH:(r + 1) * CH],
                                                start=True, stop=True)
                    last.then_inc(m2["B"], 1)
                    pe.wait_ge(m2["Cs"], k + FREE)
                    for r in range(CPB):
                        last = nc.tensor.matmul(bk67[:, r * CH:(r + 1) * CH], sel[:, n + NS, :],
                                                s3[:, r * CH:(r + 1) * CH], start=True, stop=True)
                    last.then_inc(m2["C"], 1)

                def reduce(n):
                    k = b * NS + n
                    for h in range(HV):
                        pe.wait_ge(hC_done[h], k + 1 + FREE)
                        for r in range(CPB):
                            last = nc.tensor.matmul(bank[h * CPB + r][:, :], ident[:, :], hC[:, h, r * CH:(r + 1) * CH],
                                                    start=False, stop=True, skip_group_check=True)
                        last.then_inc(reduced[h], 1)

                spread(0)
                with pe.Fori(0, NS - 1) as n:
                    spread(n + 1)
                    reduce(n)
                reduce(NS - 1)
                pe.wait_ge(m2["yg"], b + 1)
                for t in range(TPB):
                    o = bk45[:, t * P:(t + 1) * P]
                    nc.tensor.matmul(o, ones[0:1, :], bop[0:1, :], start=True, stop=False)
                    for h in range(HV):
                        last = nc.tensor.matmul(o, hC[:, h, t * P:(t + 1) * P], wop[:, h, :],
                                                start=False, stop=(h == HV - 1))
                last.then_inc(m2["op"], 1)

        def ssm2_scalar(act):
            with act.Fori(0, B) as b:
                act.wait_ge(m2["xp"], b + 1)
                nc.scalar.copy(hi3[:, :], bk45[0:KS3, :])
                nc.scalar.copy(xd[KS3:KS3 + RK, :], bk45[KS3:KS3 + RK, :]).then_inc(m2["xd"], 1)
                act.wait_ge(m2["dt"], b + 1)
                for h in range(HV):
                    for r in range(CPB):
                        last = nc.scalar.activation(ea[:, h, r * CH:(r + 1) * CH], bank[h * CPB + r][:, :], ACT.Abs,
                                                    bias=bdt[:, h:h + 1])
                last.then_inc(m2["ea"], 1)
                act.wait_ge(m2["ea"], b + 1)
                nc.scalar.activation(eb[:, :, :], ea[:, :, :], ACT.Exp, scale=-1.0).then_inc(m2["eb"], 1)
                act.wait_ge(m2["eb"], b + 1)
                nc.scalar.activation(du[:, :, :], eb[:, :, :], ACT.Ln, bias=1.0).then_inc(m2["ln"], 1)
                act.wait_ge(m2["delta"], b + 1)
                with act.Fori(0, NS) as n:
                    k = b * NS + n
                    for h in range(HV):
                        act.wait_ge(scanned[h], k + FREE)
                        nc.scalar.activation(dA[:, h, :], delta[:, h, :], ACT.Exp,
                                             scale=aneg[:, bass.ds(n + h * NS, 1)]).then_inc(dA_done[h], 1)
                    act.wait_ge(m2["C"], k + 1)
                    for h in range(HV):
                        act.wait_ge(hC_done[h], k + FREE)
                    nc.scalar.copy(Cs[:, :], bk67[:, :]).then_inc(m2["Cs"], 1)

        credited = [m1["xb"], m1["u"], m1["g"], m2["xupd"], m2["mul"], m2["Cs"]] + scanned + hC_done + reduced
        for f in (moe0, moe1, ter0, ter1):
            credited += [f.xupd, f.ssq, f.topd]

        loads = [
            (wg[:, :], Wg), (w1s[:, :], w1), (w2s[:, :, :], w2.rearrange("(k p) n -> p k n", p=P)),
            (wqkv[:, :], w_qkvT), (wo[:, :], w_outT), (bo[:, :], b_out.rearrange("(o n) -> o n", o=1)),
            (wup[:, :], upT), (wdn[:, :, :], downT.rearrange("(k p) n -> p k n", p=P)),
            (win[:, :], in_wT), (bin_[:, :], in_b),
            (cw[:, :, :], conv_w.rearrange("(h p) k -> p h k", p=P)), (cb[:, :], conv_b),
            (wdt[KS3:KS3 + RK, :], dt_wT), (bdt[:, :], dt_b),
            (alog[:, :].rearrange("p (h n) -> p h n", h=HV), A_log.rearrange("(h p) n -> p h n", p=P)),
            (dpar[:, :], D_param),
            (wop[:, :, :], op_wT.rearrange("(h p) n -> p h n", p=P)), (bop[:, :], op_b.rearrange("(o n) -> o n", o=1)),
        ]
        xpv = xp_wT.rearrange("(h p) n -> p h n", p=P)
        for r in range(3):
            loads.append((wx[:, :, r * 2 * NS:(r + 1) * 2 * NS], xpv[:, :, RK:RK + 2 * NS]))
        loads.append((wx[:, :, KS3:KS3 + RK], xpv[:, :, 0:RK]))

        block = ctx.enter_context(nc.Block())

        @block.sync
        def _(sp):
            sp.dma_start(x[:, :].rearrange("p (t d) -> p t d", d=D), x_src).then_inc(x_inp, 16)
            for dst, src in loads:
                sp.dma_start(dst, src).then_inc(w_in, 16)
            for s in credited:
                sp.sem_inc(s, FREE)
            for c in range(NC):
                sp.wait_ge(ter1.xupd, c + 1 + FREE)
                sp.dma_start(x_dst[:, c * TPC:(c + 1) * TPC, :],
                             x[:, c * CH:(c + 1) * CH].rearrange("p (t d) -> p t d", d=D)).then_inc(out_done, 16)
            sp.wait_ge(out_done, 16 * NC)

        @block.gpsimd
        def _(pool):
            link = stepper(pool, set_pool_step, 0)
            link(nc.gpsimd.memset(mhalf[:, :], -0.5))
            link(nc.gpsimd.memset(half[:, :], 0.5))
            link(nc.gpsimd.memset(mone[:, :], -1.0))
            link(nc.gpsimd.memset(lneps[:, :], LN_EPS))
            link(nc.gpsimd.memset(rmseps[:, :], RMS_EPS))
            link(nc.gpsimd.memset(ones[:, :], 1.0))
            link(nc.gpsimd.memset(ident[:, :], 0.0))
            link(nc.gpsimd.memset(identb[:, :], 0.0))
            link(nc.gpsimd.memset(qmask[:, :], HD ** -0.5))
            link(nc.gpsimd.memset(mask[:, :, :], 0.0))
            link(nc.gpsimd.memset(xw[:, :], 0.0))
            link(nc.gpsimd.memset(kT[:, :], 0.0))
            link(nc.gpsimd.memset(va[:, :, :, :], 1.0))
            link(nc.gpsimd.memset(xb[:, :, :, :], 0.0))
            link(nc.gpsimd.memset(sel[:, :, :], 0.0))
            link(nc.gpsimd.affine_select(out=ident[:, :], in_=ident[:, :], compare_op=ALU.not_equal, fill=1.0, base=0,
                                    pattern=[[-1, P]], channel_multiplier=1))
            link(nc.gpsimd.affine_select(out=identb[:, :], in_=identb[:, :], compare_op=ALU.not_equal, fill=1.0, base=0,
                                    pattern=[[-1, P]], channel_multiplier=1))
            for j in range(JG):
                rows = qmask[32 * j:32 * j + 32, :]
                link(nc.gpsimd.affine_select(out=rows, in_=rows, compare_op=ALU.is_ge, fill=0.0, base=0,
                                        pattern=[[-HD, HPG]], channel_multiplier=1))
            for r in range(3):
                link(nc.gpsimd.affine_select(out=sel[:, :, :], in_=sel[:, :, :], compare_op=ALU.not_equal, fill=1.0,
                                        base=-2 * NS * r, pattern=[[-1, 2 * NS], [0, P]], channel_multiplier=1))
            for j in range(JG):
                rows = qmask[32 * j:32 * j + 32, :]
                link(nc.gpsimd.affine_select(out=rows, in_=rows, compare_op=ALU.is_ge, fill=0.0, base=HD - 1,
                                        pattern=[[HD, HPG]], channel_multiplier=-1))
            for s in range(2):
                rows = mask[64 * s:64 * s + 64, :, :]
                link(nc.gpsimd.affine_select(out=rows, in_=rows, compare_op=ALU.is_gt, fill=MASKED, base=0,
                                        pattern=[[0, NT], [1, P]], channel_multiplier=-1))
            for s in range(2):
                rows = mask[64 * s:64 * s + 64, :, :]
                link(nc.gpsimd.affine_select(out=rows, in_=rows, compare_op=ALU.is_ge, fill=MASKED, base=64,
                                        pattern=[[0, NT], [-1, P]], channel_multiplier=1))
            for b in range(B):
                link(nc.gpsimd.memset(mask[0:64, b * TPB, 0:64], MASKED))
            last = nc.gpsimd.memset(thr[:, :], 0.0)
            last.then_inc(set_pool, 1)
            ffn_pool(pool, moe0)
            attn_pool(pool)
            ffn_pool(pool, moe1)
            ffn_pool(pool, ter0)
            ssm1_pool(pool)
            ssm2_pool(pool)
            ffn_pool(pool, ter1)

        @block.scalar
        def _(act):
            act.wait_ge(w_in, 16 * len(loads))
            nc.scalar.activation(aneg[:, :], alog[:, :], ACT.Exp).then_inc(set_act, 1)
            act.wait_ge(set_pool, 1)
            ffn_scalar(act, moe0)
            attn_scalar(act)
            ffn_scalar(act, moe1)
            ffn_scalar(act, ter0)
            ssm1_scalar(act)
            ssm2_scalar(act)
            ffn_scalar(act, ter1)

        @block.vector
        def _(dve):
            dve.wait_ge(w_in, 16 * len(loads))
            dve.wait_ge(set_pool, 1)
            link = stepper(dve, set_dve_step, 0)
            dve.wait_ge(set_act, 1)
            nc.vector.tensor_scalar(aneg[:, :], aneg[:, :], -1.0, None, ALU.mult)
            for h in range(HV):
                nc.vector.tensor_scalar(diagD[:, h, :], ident[:, :], dpar[:, h:h + 1], None, ALU.mult)
            nc.vector.tensor_reduce(asum[:, 0:1], wup[:, :], AX.X, ALU.add, apply_absolute_value=True)
            link(nc.vector.tensor_reduce(asum[:, 1:2], wdn[:, :, :], AX.XY, ALU.add, apply_absolute_value=True))
            dve.wait_ge(set_pe, 1)
            nc.vector.tensor_scalar(thr[:, 0:2], psT[:, 0:2], 0.5 / (DFF * D), None, ALU.mult)
            link(nc.vector.tensor_scalar(thr[:, 2:4], psT[:, 0:2], -0.5 / (DFF * D), None, ALU.mult))
            for i, w in enumerate((wup[:, :], wdn[:, :, :].rearrange("p k n -> p (k n)"))):
                link(nc.vector.tensor_scalar(aw[:, :], w, thr[:, i:i + 1], None, ALU.is_gt))
                link(nc.vector.scalar_tensor_tensor(out=w, in0=w, scalar=thr[:, 2 + i:3 + i], in1=aw[:, :],
                                                    op0=ALU.is_lt, op1=ALU.subtract))
                last = nc.vector.tensor_scalar(w, w, -1.0, None, ALU.mult)
            last.then_inc(set_dve, 1)
            ffn_vector(dve, moe0, x_inp, 16)
            attn_vector(dve)
            ffn_vector(dve, moe1, at["xupd"], NT)
            ffn_vector(dve, ter0, moe1.xupd, NC + FREE)
            ssm1_vector(dve)
            ssm2_vector(dve)
            ffn_vector(dve, ter1, m2["xupd"], B + FREE)

        @block.tensor
        def _(pe):
            pe.wait_ge(w_in, 16 * len(loads))
            pe.wait_ge(set_pool, 1)
            pe.wait_ge(set_dve_step, 1)
            nc.tensor.matmul(psT[:, 0:2], ones[:, :], asum[:, :], start=True, stop=True).then_inc(set_pe, 1)
            pe.wait_ge(set_dve, 1)
            ffn_tensor(pe, moe0)
            attn_tensor(pe)
            ffn_tensor(pe, moe1)
            ffn_tensor(pe, ter0)
            ssm1_tensor(pe)
            ssm2_tensor(pe)
            ffn_tensor(pe, ter1)


def kernel(**inputs):
    import numpy as _np
    import concourse.bacc as _bacc
    from concourse import mybir as _mybir
    from concourse.bass_utils import run_bass_kernel_spmd as _run

    def turned(name):
        return _np.ascontiguousarray(_np.asarray(inputs[name]).T)

    def plain(name):
        return _np.ascontiguousarray(inputs[name])

    def columns(name):
        return _np.ascontiguousarray(_np.asarray(inputs[name]).reshape(-1, P).T)

    conv = plain("L1_attn_conv_w")
    ins = [
        ("x", plain("L0_attn_x")), ("w_qkvT", turned("L0_attn_w_qkv")), ("w_outT", turned("L0_attn_w_out")),
        ("b_out", plain("L0_attn_b_out")), ("Wg", plain("L0_ffn_Wg")), ("w1", plain("L0_ffn_w1")),
        ("w2", plain("L0_ffn_w2")), ("in_wT", turned("L1_attn_in_proj_w")), ("in_b", columns("L1_attn_in_proj_b")),
        ("conv_w", conv.reshape(conv.shape[0], conv.shape[2])), ("conv_b", columns("L1_attn_conv_b")),
        ("xp_wT", turned("L1_attn_x_proj_w")), ("dt_wT", turned("L1_attn_dt_proj_w")),
        ("dt_b", columns("L1_attn_dt_proj_b")), ("A_log", plain("L1_attn_A_log")), ("D_param", columns("L1_attn_D_param")),
        ("op_wT", turned("L1_attn_out_proj_w")), ("op_b", plain("L1_attn_out_proj_b")),
        ("upT", turned("L1_ffn_w_up")), ("downT", turned("L1_ffn_w_down")),
    ]
    nc = _bacc.Bacc("TRN2", target_bir_lowering=False, num_devices=1)
    arrays = {f"in_{n}_dram": a for n, a in ins}
    args = [nc.dram_tensor(f"in_{n}_dram", a.shape, _mybir.dt.from_np(a.dtype), kind="ExternalInput").ap()
            for n, a in ins]
    x0 = ins[0][1]
    args.append(nc.dram_tensor("out_dram", x0.shape, _mybir.dt.from_np(x0.dtype), kind="ExternalOutput").ap())
    macaron_kernel(nc, *args)
    r = _run(nc, [arrays], core_ids=[0])
    return r.results[0]["out_dram"]
```

```python
from contextlib import ExitStack

import concourse.bass as bass
from concourse import mybir

F32 = mybir.dt.float32
BF16 = mybir.dt.bfloat16
ALU = mybir.AluOpType
ACT = mybir.ActivationFunctionType
AX = mybir.AxisListType

P = 128
CH = 512
TPC = CH // P
LN_EPS = 1e-5
RMS_EPS = 1e-8
F32_EPS = 1.1920928955078125e-07
MASKED = -1.0e30
FREE = 2


def macaron_kernel(nc, x_in, w_qkvT, w_outT, b_out, Wg, w1, w2, in_wT, in_b, conv_w, conv_b,
                   xp_wT, dt_wT, dt_b, A_log, D_param, op_wT, op_b, upT, downT, out):
    B, L, D = x_in.shape
    T = B * L
    NT = T // P
    NC = T // CH
    TPB = L // P
    E = Wg.shape[1]
    DFF = w1.shape[1]
    KB = DFF // P
    H, HD, WIN = 16, 8, 64
    JG = 4
    HPG = H // JG
    DI = in_wT.shape[1] // 2
    HV = DI // P
    DC = conv_w.shape[1]
    NS = A_log.shape[1]
    RK = dt_wT.shape[0]
    KS3 = 3 * 2 * NS

    x_src = x_in.rearrange("b (t p) d -> p (b t) d", p=P)
    x_dst = out.rearrange("b (t p) d -> p (b t) d", p=P)

    with ExitStack() as ctx:
        def sb(name, shape, dt=F32):
            return ctx.enter_context(nc.sbuf_tensor(name, shape, dt))

        def sem(name):
            return ctx.enter_context(nc.semaphore(name))

        x = sb("x", [P, NT * D])
        wqkv = sb("wqkv", [P, 3 * P])
        wo = sb("wo", [P, P])
        bo = sb("bo", [1, P])
        wg = sb("wg", [P, E])
        w1s = sb("w1s", [P, DFF])
        w2s = sb("w2s", [P, KB, P])
        wup = sb("wup", [P, DFF])
        wdn = sb("wdn", [P, KB, P])
        win = sb("win", [P, 2 * DI])
        bin_ = sb("bin_", [P, 2 * HV])
        cw = sb("cw", [P, HV, DC])
        cb = sb("cb", [P, HV])
        wx = sb("wx", [P, HV, KS3 + RK])
        wdt = sb("wdt", [P, DI])
        bdt = sb("bdt", [P, HV])
        alog = sb("alog", [P, HV * NS])
        aneg = sb("aneg", [P, HV * NS])
        dpar = sb("dpar", [P, HV])
        wop = sb("wop", [P, HV, P])
        bop = sb("bop", [1, P])
        ident = sb("ident", [P, P])
        identb = sb("identb", [P, P], BF16)
        ones = sb("ones", [P, P])
        mask = sb("mask", [P, NT, P], BF16)
        qmask = sb("qmask", [P, HPG])
        sel = sb("sel", [KS3, 2 * NS, P], BF16)
        diagD = sb("diagD", [P, HV, P])
        half = sb("half", [P, H])
        lneps = sb("lneps", [P, TPC])
        zeros = sb("zeros", [P, TPC])
        lnpow = sb("lnpow", [P, 2 * TPC])
        carrier = sb("carrier", [P, 64])
        stats = sb("stats", [P, TPC, 6])
        mv = sb("mv", [P, TPC, 2])
        veps = sb("veps", [P, 2 * TPC])
        powers = sb("powers", [P, 2 * TPC])
        sd = sb("sd", [P, TPC])
        rr = sb("rr", [P, TPC])
        nscale = sb("nscale", [P, TPC])
        xn = sb("xn", [P, CH])
        xT = sb("xT", [P, CH])
        hT = sb("hT", [P, KB, CH])
        hsq = sb("hsq", [P, KB, CH])
        top = sb("top", [P, TPC, 8])
        topd = sb("topd", [P, TPC, 8])
        tope = sb("tope", [P, TPC, 8])
        gz = sb("gz", [P, 8, TPC])
        g12 = sb("g12", [P, TPC, 2])
        gn = sb("gn", [P, TPC, 2])
        gs = sb("gs", [P, TPC])
        aw = sb("aw", [P, DFF])
        asum = sb("asum", [P, 2])
        thr = sb("thr", [P, 4])
        xw = sb("xw", [P, P // 2 + P])
        qm = sb("qm", [P, HPG, P])
        kT = sb("kT", [P, P // 2 + P])
        va = sb("va", [P, 2, H, HD + 1])
        ssub = sb("ssub", [P, JG, HPG * P])
        pT = sb("pT", [P, 2, HPG * P])
        smax = sb("smax", [P, H])
        rden = sb("rden", [P, H])
        cx = sb("cx", [P, H, HD])
        cxT = sb("cxT", [P, P])
        xb = sb("xb", [P, 2, HV, DC - 1 + CH])
        cacc = sb("cacc", [P, HV, CH])
        u = sb("u", [P, HV, T])
        g = sb("g", [P, HV, T])
        s3 = sb("s3", [KS3, L], BF16)
        hi3 = sb("hi3", [KS3, L], BF16)
        r3 = sb("r3", [KS3, L])
        xd = sb("xd", [P, L])
        delta = sb("delta", [P, HV, L])
        ea = sb("ea", [P, HV, L])
        eb = sb("eb", [P, HV, L])
        du = sb("du", [P, HV, L])
        dBu = sb("dBu", [P, HV, L])
        dA = [sb("dA", [P, HV, L]), ea]
        hst = [sb("hst", [P, HV, L]), eb]
        hC = sb("hC", [P, HV, L])
        Cs = sb("Cs", [P, 2, L])

        bank = [ctx.enter_context(nc.psum_tensor(f"bank{i}", [P, 512], F32)) for i in range(4)]
        bk45 = ctx.enter_context(nc.psum_tensor("bk45", [P, 1024], F32))
        bk67 = ctx.enter_context(nc.psum_tensor("bk67", [P, 1024], F32))
        psT, psD = bk45[:, 0:512], bk45[:, 512:1024]
        psG, psQ = bk67[:, 0:512], bk67[:, 512:1024]

        w_in = sem("w_in")
        x_inp = sem("x_inp")
        w_moe = sem("w_moe")
        set_pool = sem("set_pool")
        set_attn = sem("set_attn")
        set_ssm = sem("set_ssm")
        set_pool_step = sem("set_pool_step")
        set_pe = sem("set_pe")
        set_act = sem("set_act")
        set_dve = sem("set_dve")
        set_dve_step = sem("set_dve_step")
        out_done = sem("out_done")

        def layer_norm_semaphores(name, ternary=False):
            return {
                "stats": sem(name + "_stats"),
                "ln_step": sem(name + "_lnstep"),
                "nscale": sem(name + "_nscale") if ternary else None,
                "veps": sem(name + "_veps"),
                "rstd": sem(name + "_rstd"),
                "xn": sem(name + "_xn"),
                "xpose": sem(name + "_xpose"),
            }

        class Ffn:

            def __init__(self, name, ternary, w_up, w_down, func):
                self.ternary, self.w_up, self.w_down, self.func = ternary, w_up, w_down, func
                self.ln = layer_norm_semaphores(name, ternary)
                self.xn, self.xpose = self.ln["xn"], self.ln["xpose"]
                self.xT = sem(name + "_xT")
                self.up = sem(name + "_up")
                self.h = sem(name + "_h")
                self.gstep = sem(name + "_gstep")
                self.down = sem(name + "_down")
                self.xupd = sem(name + "_xupd")
                if ternary:
                    self.hsq = sem(name + "_hsq")
                    self.ssq = sem(name + "_ssq")
                    self.gsum = sem(name + "_gsum")
                    self.rms = sem(name + "_rms")
                else:
                    self.logit = sem(name + "_logit")
                    self.topd = sem(name + "_topd")
                    self.tope = sem(name + "_tope")
                    self.scale = sem(name + "_scale")

        moe0 = Ffn("moe0", False, w1s, w2s, ACT.Relu)
        moe1 = Ffn("moe1", False, w1s, w2s, ACT.Relu)
        ter0 = Ffn("ter0", True, wup, wdn, ACT.Gelu)
        ter1 = Ffn("ter1", True, wup, wdn, ACT.Gelu)

        at = {k: sem("at_" + k) for k in (
            "xw", "xsh", "qkv", "qk", "v", "s", "max", "sub",
            "p", "pt", "pts", "pvg", "pv", "rden", "cx", "cxt", "cxs", "op", "xupd", "ksh")} | layer_norm_semaphores("at")
        m1 = {k: sem("m1_" + k) for k in (
            "xT", "proj", "xb", "cstep", "conv", "u", "g")} | layer_norm_semaphores("m1")
        m2 = {k: sem("m2_" + k) for k in (
            "xp", "s3step", "r3", "xd", "dt", "ea", "eb", "ln", "dstep", "delta",
            "B", "C", "Cs", "mul", "yg", "op", "xupd")}
        dA_done = [sem(f"dA_done{h}") for h in range(HV)]
        scanned = [sem(f"scanned{h}") for h in range(HV)]
        hC_done = [sem(f"hC_done{h}") for h in range(HV)]
        reduced = [sem(f"reduced{h}") for h in range(HV)]

        def xs(tok0, n):
            return x[:, bass.ds(tok0, n)]

        carried = [0]

        def carry_wait_vector():
            carried[0] += 1
            nc.vector.tensor_copy(carrier[:, carried[0]:carried[0] + 1], half[:, 0:1])

        def stepper(eng, s, base):
            count = [0]

            def link(ins):
                count[0] += 1
                ins.then_inc(s, 1)
                eng.wait_ge(s, base + count[0])
            return link

        LN_DVE = {False: 1, True: 4}

        def ln_stats(dve, r, idx, tok0, nt, ternary):
            link = stepper(dve, r["ln_step"], idx * LN_DVE[ternary])
            for i in range(nt):
                last = nc.vector.bn_stats(stats[:, i, :], xs(tok0 + i * D, D))
            link(last)
            carry_wait_vector()
            for i in range(nt):
                last = nc.vector.bn_aggr(mv[:, i, :], stats[:, i, :])
            last.then_inc(r["stats"], 1)

        def ln_apply(dve, r, idx, tok0, nt, ternary):
            dve.wait_ge(r["rstd"], idx + 1)
            scale = powers[:, 0:nt]
            if ternary:
                link = stepper(dve, r["ln_step"], idx * LN_DVE[ternary] + 1)
                link(nc.vector.tensor_tensor(rr[:, 0:nt], powers[:, TPC:TPC + nt], powers[:, 0:nt], ALU.mult))
                carry_wait_vector()
                nc.vector.tensor_scalar(rr[:, 0:nt], rr[:, 0:nt], RMS_EPS, None, ALU.add).then_inc(r["ln_step"], 1)
                dve.wait_ge(r["ln_step"], idx * LN_DVE[ternary] + 3)
                nc.vector.reciprocal(sd[:, 0:nt], rr[:, 0:nt]).then_inc(r["ln_step"], 1)
                dve.wait_ge(r["ln_step"], idx * LN_DVE[ternary] + 4)
                scale = nscale[:, 0:nt]
                nc.vector.tensor_tensor(scale, powers[:, 0:nt], sd[:, 0:nt], ALU.mult).then_inc(r["nscale"], 1)
                dve.wait_ge(r["nscale"], idx + 1)
            if not isinstance(idx, int) or idx > 0:
                dve.wait_ge(r["xpose"], idx)
            for i in range(nt):
                last = nc.vector.tensor_scalar(xn[:, i * D:(i + 1) * D], xs(tok0 + i * D, D), mv[:, i, 0:1],
                                               scale[:, i:i + 1], ALU.subtract, ALU.mult)
            last.then_inc(r["xn"], 1)

        def ln_pool(pool, r, idx, nt, ternary):
            pool.wait_ge(r["stats"], idx + 1)
            last = nc.gpsimd.tensor_tensor(veps[:, 0:nt], mv[:, 0:nt, 1], lneps[:, 0:nt], ALU.add)
            n = nt
            if ternary:
                last = nc.gpsimd.tensor_tensor(veps[:, TPC:2 * TPC], mv[:, :, 1], zeros[:, 0:TPC], ALU.add)
                n = 2 * TPC
            last.then_inc(r["veps"], 1)
            pool.wait_ge(r["veps"], idx + 1)
            nc.gpsimd.tensor_tensor(powers[:, 0:n], veps[:, 0:n], lnpow[:, 0:n], ALU.pow).then_inc(r["rstd"], 1)

        def ffn_vector(dve, f, before, count):
            dve.wait_ge(before, count)

            def gate(c):
                link = stepper(dve, f.gstep, c * 8)
                dve.wait_ge(f.logit, c + 1)
                carry_wait_vector()
                for i in range(TPC):
                    last = nc.vector.max(top[:, i, :], psG[:, i * 8:(i + 1) * 8])
                link(last)
                nc.vector.tensor_tensor(topd[:, :, :], top[:, :, :], top[:, :, 0:1].to_broadcast([P, TPC, 8]),
                                        ALU.subtract).then_inc(f.topd, 1)
                dve.wait_ge(f.tope, c + 1)
                link(nc.vector.tensor_reduce(gz[:, 0, :], tope[:, :, :], AX.X, ALU.add))
                link(nc.vector.reciprocal(gz[:, 1, :], gz[:, 0, :]))
                link(nc.vector.tensor_tensor(g12[:, :, :], tope[:, :, 0:2],
                                             gz[:, 1, :].rearrange("p (i o) -> p i o", o=1).to_broadcast([P, TPC, 2]),
                                             ALU.mult))
                link(nc.vector.tensor_tensor(gz[:, 2, :], g12[:, :, 0], g12[:, :, 1], ALU.add))
                link(nc.vector.tensor_scalar(gz[:, 3, :], gz[:, 2, :], F32_EPS, 2.0, ALU.max, ALU.mult))
                link(nc.vector.reciprocal(gz[:, 4, :], gz[:, 3, :]))
                link(nc.vector.tensor_tensor(gn[:, :, :], g12[:, :, :],
                                             gz[:, 4, :].rearrange("p (i o) -> p i o", o=1).to_broadcast([P, TPC, 2]),
                                             ALU.mult))
                nc.vector.tensor_tensor(gs[:, :], gn[:, :, 0], gn[:, :, 1], ALU.add).then_inc(f.scale, 1)

            def rms(c):
                link = stepper(dve, f.gstep, c * 2)
                dve.wait_ge(f.ssq, c + 1 + FREE)
                nc.vector.tensor_scalar(gz[:, 0, :], psG[:, 0:TPC], 1.0 / DFF, None, ALU.mult).then_inc(f.gsum, 1)
                dve.wait_ge(f.rms, c + 1)
                link(nc.vector.tensor_scalar(gz[:, 2, :], gz[:, 1, :], RMS_EPS, 2.0, ALU.add, ALU.mult))
                link(nc.vector.reciprocal(gs[:, :], gz[:, 2, :]))

            def update(c):
                dve.wait_ge(f.down, c + 1)
                if not f.ternary:
                    dve.wait_ge(f.scale, c + 1)
                for i in range(TPC):
                    at_ = c * CH + i * D
                    last = nc.vector.scalar_tensor_tensor(out=xs(at_, D), in0=psD[:, i * D:(i + 1) * D],
                                                          scalar=gs[:, i:i + 1], in1=xs(at_, D),
                                                          op0=ALU.mult, op1=ALU.add)
                last.then_inc(f.xupd, 1)

            side = rms if f.ternary else gate
            t_ = f.ternary
            ln_stats(dve, f.ln, 0, 0, TPC, t_)
            ln_apply(dve, f.ln, 0, 0, TPC, t_)
            ln_stats(dve, f.ln, 1, CH, TPC, t_)
            with dve.Fori(0, NC - 2) as c:
                ln_apply(dve, f.ln, c + 1, c * CH + CH, TPC, t_)
                ln_stats(dve, f.ln, c + 2, c * CH + 2 * CH, TPC, t_)
                side(c)
                update(c)
            ln_apply(dve, f.ln, NC - 1, (NC - 1) * CH, TPC, t_)
            for c in range(NC - 2, NC):
                side(c)
                update(c)

        def ffn_pool(pool, f):
            def squares(c):
                for k in range(KB):
                    pool.wait_ge(f.h, c * KB + k + 1)
                    if not isinstance(c, int) or c > 0:
                        pool.wait_ge(f.ssq, c + FREE)
                    nc.gpsimd.tensor_tensor(hsq[:, k, :], hT[:, k, :], hT[:, k, :], ALU.mult).then_inc(f.hsq, 1)

            def root(c):
                pool.wait_ge(f.gsum, c + 1)
                nc.gpsimd.tensor_tensor(gz[:, 1, :], gz[:, 0, :], half[:, 0:TPC], ALU.pow).then_inc(f.rms, 1)

            ln_pool(pool, f.ln, 0, TPC, f.ternary)
            ln_pool(pool, f.ln, 1, TPC, f.ternary)
            with pool.Fori(0, NC - 2) as c:
                if f.ternary:
                    squares(c)
                ln_pool(pool, f.ln, c + 2, TPC, f.ternary)
                if f.ternary:
                    root(c)
            if f.ternary:
                for c in range(NC - 2, NC):
                    squares(c)
                    root(c)

        def transposes(pe, xn_s, xpose_s, xT_s, idx):
            pe.wait_ge(xn_s, idx + 1)
            if not isinstance(idx, int) or idx > 0:
                pe.wait_ge(xT_s, idx)
            for i in range(TPC):
                last = nc.tensor.transpose(psT[:, i * P:(i + 1) * P], xn[:, i * P:(i + 1) * P], ident[:, :])
            last.then_inc(xpose_s, 1)

        def ffn_tensor(pe, f):
            def up(c):
                pe.wait_ge(f.xT, c + 1)
                if not f.ternary:
                    if not isinstance(c, int) or c > 0:
                        pe.wait_ge(f.topd, c + FREE)
                    for i in range(TPC):
                        last = nc.tensor.matmul(psG[:, i * 8:(i + 1) * 8], xT[:, i * P:(i + 1) * P], wg[:, :],
                                                start=True, stop=True)
                    last.then_inc(f.logit, 1)
                for k in range(KB):
                    nc.tensor.matmul(bank[k][:, :], f.w_up[:, k * P:(k + 1) * P], xT[:, :],
                                     start=True, stop=True).then_inc(f.up, 1)

            def down(c):
                if not isinstance(c, int) or c > 0:
                    pe.wait_ge(f.xupd, c + FREE)
                for k in range(KB):
                    pe.wait_ge(f.h, c * KB + k + 1)
                    for i in range(TPC):
                        last = nc.tensor.matmul(psD[:, i * P:(i + 1) * P], hT[:, k, i * P:(i + 1) * P],
                                                f.w_down[:, k, :], start=(k == 0 and i == 0), stop=(k == KB - 1),
                                                skip_group_check=True)
                last.then_inc(f.down, 1)
                if f.ternary:
                    for k in range(KB):
                        pe.wait_ge(f.hsq, c * KB + k + 1)
                        for i in range(TPC):
                            last = nc.tensor.matmul(psG[:, i:i + 1], hsq[:, k, i * P:(i + 1) * P], ones[:, 0:1],
                                                    start=(k == 0 and i == 0), stop=(k == KB - 1),
                                                    skip_group_check=True)
                    last.then_inc(f.ssq, 1)

            transposes(pe, f.xn, f.xpose, f.xT, 0)
            with pe.Fori(0, NC - 1) as c:
                up(c)
                transposes(pe, f.xn, f.xpose, f.xT, c + 1)
                down(c)
            up(NC - 1)
            down(NC - 1)

        def copy_xT(act, xpose_s, xT_s, used_s, used, idx):
            act.wait_ge(xpose_s, idx + 1)
            if not isinstance(idx, int) or idx > 0:
                act.wait_ge(used_s, used)
            nc.scalar.copy(xT[:, :], psT).then_inc(xT_s, 1)

        def ffn_scalar(act, f):
            def hidden(c):
                for k in range(KB):
                    act.wait_ge(f.up, c * KB + k + 1)
                    nc.scalar.activation(hT[:, k, :], bank[k][:, :], f.func).then_inc(f.h, 1)

            def gate(c):
                act.wait_ge(f.topd, c + 1 + FREE)
                nc.scalar.activation(tope[:, :, :], topd[:, :, :], ACT.Exp).then_inc(f.tope, 1)

            if f.ternary:
                nc.scalar.preload_act_table(f.func)
            copy_xT(act, f.xpose, f.xT, f.up, 0, 0)
            with act.Fori(0, NC - 1) as c:
                hidden(c)
                copy_xT(act, f.xpose, f.xT, f.up, (c + 1) * KB, c + 1)
                if not f.ternary:
                    gate(c)
            hidden(NC - 1)
            if not f.ternary:
                gate(NC - 1)

        def over_tiles(eng, body):
            body(0, True, False)
            with eng.Fori(1, NT - 1) as t:
                body(t, False, False)
            body(NT - 1, False, True)

        def attn_vector(dve):
            dve.wait_ge(moe0.xupd, NC + FREE)
            psO = psD[:, 0:H * (HD + 1)].rearrange("p (h e) -> p h e", e=HD + 1)
            psP = psD[:, 160:160 + P]

            def ln(t):
                ln_stats(dve, at, t, t * D, 1, False)
                ln_apply(dve, at, t, t * D, 1, False)

            def context(t):
                dve.wait_ge(at["pv"], t + 1)
                nc.vector.reciprocal(rden[:, :], psO[:, :, HD]).then_inc(at["rden"], 1)
                dve.wait_ge(at["rden"], t + 1)
                nc.vector.tensor_tensor(cx[:, :, :], psO[:, :, 0:HD],
                                        rden[:, :].rearrange("p (h o) -> p h o", o=1).to_broadcast([P, H, HD]),
                                        ALU.mult).then_inc(at["cx"], 1)

            def soften(t, j):
                s3d = bank[j][:, :].rearrange("p (a k) -> p a k", a=HPG)
                dve.wait_ge(at["s"], t * JG + j + 1)
                nc.vector.tensor_reduce(smax[:, j * HPG:(j + 1) * HPG], s3d, AX.X, ALU.max).then_inc(at["max"], 1)
                dve.wait_ge(at["max"], t * JG + j + 1)
                m = smax[:, j * HPG:(j + 1) * HPG].rearrange("p (a o) -> p a o", o=1).to_broadcast([P, HPG, P])
                if not isinstance(t, int) or t > 0:
                    dve.wait_ge(at["pt"], t * JG - JG + j + 1)
                nc.vector.tensor_tensor(ssub[:, j, :].rearrange("p (a k) -> p a k", a=HPG), s3d, m,
                                        ALU.subtract).then_inc(at["sub"], 1)

            def update(t):
                dve.wait_ge(at["op"], t + 1)
                nc.vector.tensor_tensor(xs(t * D, D), psP, xs(t * D, D), ALU.add).then_inc(at["xupd"], 1)

            def body(t, first, last):
                if not first:
                    context(t - 1)
                if not last:
                    ln(t + 1)
                soften(t, 0)
                if not first:
                    update(t - 1)
                for j in range(1, JG):
                    soften(t, j)

            ln(0)
            over_tiles(dve, body)
            context(NT - 1)
            update(NT - 1)

        def attn_pool(pool):
            with pool.Fori(0, NT) as t:
                ln_pool(pool, at, t, 1, False)

        def attn_tensor(pe):
            psO = psD[:, 0:H * (HD + 1)].rearrange("p (h e) -> p h e", e=HD + 1)
            psP = psD[:, 160:160 + P]
            psX = psD[:, 288:288 + P]
            psPT = [psT, psG]

            def xpose(t):
                pe.wait_ge(at["xn"], t + 1)
                if not isinstance(t, int) or t > 1:
                    pe.wait_ge(at["xupd"], t - 1)
                nc.tensor.transpose(psX, xn[:, 0:P], ident[:, :]).then_inc(at["xpose"], 1)

            def qkv(t):
                pe.wait_ge(at["xw"], t + 1)
                if not isinstance(t, int) or t > 0:
                    pe.wait_ge(at["qk"], t)
                    pe.wait_ge(at["v"], t)
                for n in range(2):
                    nc.tensor.matmul(psQ[:, n * P:(n + 1) * P], wqkv[:, n * P:(n + 1) * P], xw[:, 64:64 + P],
                                     start=True, stop=True)
                for s in range(2):
                    last = nc.tensor.matmul(psQ[:, (2 + s) * P:(3 + s) * P], xw[:, 64 * s:64 * s + P],
                                            wqkv[:, 2 * P:3 * P], start=True, stop=True)
                last.then_inc(at["qkv"], 1)

            def scores(t, j):
                if j == 0:
                    pe.wait_ge(at["qk"], t + 1)
                if not isinstance(t, int) or t > 0:
                    pe.wait_ge(at["sub"], t * JG - JG + j + 1)
                for a in range(HPG):
                    nc.tensor.matmul(bank[j][:, a * P:(a + 1) * P], identb[:, :], mask[:, t, :],
                                     start=(a == 0), stop=False, skip_group_check=True)
                for a in range(HPG):
                    for s in range(2):
                        last = nc.tensor.matmul(bank[j][64 * s:64 * s + 64, a * P:(a + 1) * P],
                                                qm[32 * j:32 * j + 32, a, 64 * s:64 * s + 64],
                                                kT[32 * j:32 * j + 32, 64 * s:64 * s + P],
                                                start=False, stop=True, skip_group_check=True)
                last.then_inc(at["s"], 1)

            def prob_t(t, j):
                pe.wait_ge(at["p"], t * JG + j + 1)
                if j >= 2:
                    pe.wait_ge(at["pts"], t * JG + j - 1)
                elif not isinstance(t, int) or t > 0:
                    pe.wait_ge(at["pts"], t * JG + j - 1)
                for a in range(HPG):
                    last = nc.tensor.transpose(psPT[j % 2][:, a * P:(a + 1) * P], ssub[:, j, a * P:(a + 1) * P],
                                               ident[:, :])
                last.then_inc(at["pt"], 1)

            def values(t, j):
                pe.wait_ge(at["pts"], t * JG + j + 1)
                if j == 0:
                    pe.wait_ge(at["v"], t + 1)
                    if not isinstance(t, int) or t > 0:
                        pe.wait_ge(at["xupd"], t)
                for a in range(HPG):
                    h = j * HPG + a
                    for s in range(2):
                        last = nc.tensor.matmul(psO[64 * s:64 * s + 64, h, :],
                                                pT[:, j % 2, a * P + 64 * s:a * P + 64 * s + 64],
                                                va[:, s, h, :], start=True, stop=True)
                if j == JG - 1:
                    last.then_inc(at["pv"], 1)
                else:
                    last.then_inc(at["pvg"], 1)

            def body(t, first, last):
                scores(t, 0)
                if not first:
                    ctx_t(t - 1)
                scores(t, 1)
                if not first:
                    project(t - 1)
                scores(t, 2)
                if not last:
                    xpose(t + 1)
                scores(t, 3)
                if not last:
                    qkv(t + 1)
                prob_t(t, 0)
                prob_t(t, 1)
                values(t, 0)
                prob_t(t, 2)
                values(t, 1)
                prob_t(t, 3)
                values(t, 2)
                values(t, 3)

            def ctx_t(t):
                pe.wait_ge(at["cx"], t + 1)
                nc.tensor.transpose(psX, cx[:, :, :].rearrange("p h e -> p (h e)"), ident[:, :]).then_inc(at["cxt"], 1)

            def project(t):
                pe.wait_ge(at["cxs"], t + 1)
                nc.tensor.matmul(psP, cxT[:, :], wo[:, :], start=True, stop=False)
                nc.tensor.matmul(psP, ones[0:1, :], bo[0:1, :], start=False, stop=True).then_inc(at["op"], 1)

            xpose(0)
            qkv(0)
            over_tiles(pe, body)
            ctx_t(NT - 1)
            project(NT - 1)

        def attn_scalar(act):
            psX = psD[:, 288:288 + P]
            psPT = [psT, psG]

            def copy_x(t):
                if not isinstance(t, int) or t > 0:
                    act.wait_ge(at["qkv"], t)
                    nc.scalar.copy(xw[:, 0:64], xw[:, P:P + 64]).then_inc(at["xsh"], 1)
                    act.wait_ge(at["xsh"], t)
                act.wait_ge(at["xpose"], t + 1)
                nc.scalar.copy(xw[:, 64:64 + P], psX).then_inc(at["xw"], 1)

            def copy_qk(t):
                act.wait_ge(at["qkv"], t + 1)
                if not isinstance(t, int) or t > 0:
                    act.wait_ge(at["s"], t * JG)
                    nc.scalar.copy(kT[:, 0:64], kT[:, P:P + 64]).then_inc(at["ksh"], 1)
                for a in range(HPG):
                    nc.scalar.activation(qm[:, a, :], psQ[:, 0:P], ACT.Copy, scale=qmask[:, a:a + 1])
                if not isinstance(t, int) or t > 0:
                    act.wait_ge(at["ksh"], t)
                nc.scalar.copy(kT[:, 64:64 + P], psQ[:, P:2 * P]).then_inc(at["qk"], 1)

            def copy_v(t):
                act.wait_ge(at["qkv"], t + 1)
                if not isinstance(t, int) or t > 0:
                    act.wait_ge(at["pv"], t)
                nc.scalar.copy(va[:, :, :, 0:HD], psQ[:, 2 * P:4 * P].rearrange("p (s h e) -> p s h e", s=2, e=HD)
                               ).then_inc(at["v"], 1)

            def probs(t, j):
                act.wait_ge(at["sub"], t * JG + j + 1)
                nc.scalar.activation(ssub[:, j, :], ssub[:, j, :], ACT.Exp).then_inc(at["p"], 1)

            def probs_t(t, j):
                act.wait_ge(at["pt"], t * JG + j + 1)
                if j >= 2:
                    act.wait_ge(at["pvg"], t * (JG - 1) + j - 1)
                elif not isinstance(t, int) or t > 0:
                    act.wait_ge(at["pv"], t)
                nc.scalar.copy(pT[:, j % 2, :], psPT[j % 2]).then_inc(at["pts"], 1)

            def body(t, first, last):
                copy_v(t)
                if not first:
                    copy_ctx(t - 1)
                probs(t, 0)
                if not last:
                    copy_x(t + 1)
                for j in range(1, JG):
                    probs(t, j)
                probs_t(t, 0)
                probs_t(t, 1)
                if not last:
                    copy_qk(t + 1)
                probs_t(t, 2)
                probs_t(t, 3)

            def copy_ctx(t):
                act.wait_ge(at["cxt"], t + 1)
                nc.scalar.copy(cxT[:, :], psX).then_inc(at["cxs"], 1)

            copy_x(0)
            copy_qk(0)
            over_tiles(act, body)
            copy_ctx(NT - 1)

        
        CPB = L // CH
        PROJ = 2 * HV

        def ssm1_vector(dve):
            dve.wait_ge(ter0.xupd, NC + FREE)

            def ln(c):
                ln_stats(dve, m1, c, c * CH, TPC, False)
                ln_apply(dve, m1, c, c * CH, TPC, False)

            def conv(c, r):
                link = stepper(dve, m1["cstep"], c * (DC - 1))
                dve.wait_ge(m1["xb"], (c + 1) * HV + FREE)
                if not isinstance(c, int) or c > 0:
                    dve.wait_ge(m1["u"], c + FREE)
                for k in range(DC):
                    for h in range(HV):
                        src = xb[:, r, h, k:k + CH]
                        if k == 0:
                            last = nc.vector.tensor_scalar(cacc[:, h, :], src, cw[:, h, k:k + 1], cb[:, h:h + 1],
                                                           ALU.mult, ALU.add)
                        else:
                            last = nc.vector.scalar_tensor_tensor(out=cacc[:, h, :], in0=src, scalar=cw[:, h, k:k + 1],
                                                                  in1=cacc[:, h, :], op0=ALU.mult, op1=ALU.add)
                    if k < DC - 1:
                        link(last)
                last.then_inc(m1["conv"], 1)

            ln(0)
            with dve.Fori(0, B - 1) as b:
                for r in range(CPB):
                    ln(b * CPB + r + 1)
                    conv(b * CPB + r, r)
            c0 = (B - 1) * CPB
            for r in range(CPB):
                if r < CPB - 1:
                    ln(c0 + r + 1)
                conv(c0 + r, r)

        def ssm1_pool(pool):
            with pool.Fori(0, NC) as c:
                ln_pool(pool, m1, c, TPC, False)

        def ssm1_tensor(pe):
            def proj(c):
                pe.wait_ge(m1["xT"], c + 1)
                if not isinstance(c, int) or c > 0:
                    pe.wait_ge(m1["xb"], c * HV + FREE)
                    pe.wait_ge(m1["g"], c + FREE)
                for k in range(PROJ):
                    nc.tensor.matmul(bank[k][:, :], win[:, k * P:(k + 1) * P], xT[:, :],
                                     start=True, stop=True).then_inc(m1["proj"], 1)

            transposes(pe, m1["xn"], m1["xpose"], m1["xT"], 0)
            with pe.Fori(0, NC - 1) as c:
                proj(c)
                transposes(pe, m1["xn"], m1["xpose"], m1["xT"], c + 1)
            proj(NC - 1)

        def ssm1_scalar(act):
            def chunk(c, r, last):
                if r > 0:
                    act.wait_ge(m1["xb"], c * HV + FREE)
                    for h in range(HV):
                        i = nc.scalar.copy(xb[:, r, h, 0:DC - 1], xb[:, r - 1, h, CH:CH + DC - 1])
                for h in range(HV):
                    act.wait_ge(m1["proj"], c * PROJ + h + 1)
                    nc.scalar.activation(xb[:, r, h, DC - 1:], bank[h][:, :], ACT.Identity,
                                         bias=bin_[:, h:h + 1]).then_inc(m1["xb"], 1)
                act.wait_ge(m1["proj"], (c + 1) * PROJ)
                for h in range(HV):
                    i = nc.scalar.activation(g[:, h, bass.ds(c * CH, CH)], bank[HV + h][:, :], ACT.Silu,
                                             bias=bin_[:, HV + h:HV + h + 1])
                i.then_inc(m1["g"], 1)
                if not last:
                    copy_xT(act, m1["xpose"], m1["xT"], m1["proj"], (c + 1) * PROJ, c + 1)
                act.wait_ge(m1["conv"], c + 1)
                for h in range(HV):
                    i = nc.scalar.activation(u[:, h, bass.ds(c * CH, CH)], cacc[:, h, :], ACT.Silu)
                i.then_inc(m1["u"], 1)

            nc.scalar.preload_act_table(ACT.Silu)
            copy_xT(act, m1["xpose"], m1["xT"], m1["proj"], 0, 0)
            with act.Fori(0, B - 1) as b:
                for r in range(CPB):
                    chunk(b * CPB + r, r, False)
            for r in range(CPB):
                chunk((B - 1) * CPB + r, r, r == CPB - 1)

        def ssm2_vector(dve):
            with dve.Fori(0, B) as b:
                link = stepper(dve, m2["s3step"], b * 3)
                dve.wait_ge(m2["xd"], b + 1)
                link(nc.vector.tensor_tensor(r3[:, :], bk45[0:KS3, :], hi3[:, :], ALU.subtract))
                nc.vector.tensor_copy(s3[2 * NS:4 * NS, :], r3[2 * NS:4 * NS, :])
                link(nc.vector.tensor_copy(hi3[4 * NS:KS3, :], r3[4 * NS:KS3, :]))
                link(nc.vector.tensor_tensor(s3[4 * NS:KS3, :], r3[4 * NS:KS3, :], hi3[4 * NS:KS3, :], ALU.subtract))
                nc.vector.tensor_copy(s3[0:2 * NS, :], hi3[0:2 * NS, :]).then_inc(m2["r3"], 1)
                link = stepper(dve, m2["dstep"], b * 5)
                dve.wait_ge(m2["ea"], b + 1)
                for h in range(HV):
                    for r in range(CPB):
                        last = nc.vector.tensor_scalar(delta[:, h, r * CH:(r + 1) * CH], bank[h * CPB + r][:, :],
                                                       bdt[:, h:h + 1], 0.0, ALU.add, ALU.max)
                link(last)
                dve.wait_ge(m2["eb"], b + 1)
                link(nc.vector.tensor_scalar(ea[:, :, :], eb[:, :, :], 1.0, -1.0, ALU.add, ALU.add))
                dve.wait_ge(m2["ln"], b + 1)
                link(nc.vector.tensor_tensor(delta[:, :, :], delta[:, :, :], du[:, :, :], ALU.add))
                link(nc.vector.tensor_tensor(eb[:, :, :], eb[:, :, :], ea[:, :, :], ALU.subtract))
                link(nc.vector.tensor_tensor(delta[:, :, :], delta[:, :, :], eb[:, :, :], ALU.add))
                nc.vector.tensor_tensor(du[:, :, :], delta[:, :, :], u[:, :, bass.ds(b * L, L)],
                                        ALU.mult).then_inc(m2["delta"], 1)
                dve.wait_ge(m2["delta"], b + 1)
                carry_wait_vector()
                with dve.Fori(0, NS // 2) as pair:
                    for q in range(2):
                        k = b * NS + pair * 2 + q
                        dve.wait_ge(m2["B"], k + 1)
                        for h in range(HV):
                            dve.wait_ge(scanned[h], k + FREE)
                            nc.vector.tensor_tensor(dBu[:, h, :], bk45[:, :], du[:, h, :], ALU.mult
                                                    ).then_inc(m2["mul"], 1)
                        for h in range(HV):
                            dve.wait_ge(m2["mul"], k * HV + h + 1 + FREE)
                            dve.wait_ge(dA_done[h], k + 1)
                            dve.wait_ge(hC_done[h], k - 1 + FREE)
                            nc.vector.tensor_tensor_scan(hst[q][:, h, :], dA[q][:, h, :], dBu[:, h, :], 0.0,
                                                         ALU.mult, ALU.add).then_inc(scanned[h], 1)
                for h in range(HV):
                    dve.wait_ge(reduced[h], (b + 1) * NS + FREE)
                    for r in range(CPB):
                        last = nc.vector.tensor_tensor(hC[:, h, r * CH:(r + 1) * CH], bank[h * CPB + r][:, :],
                                                       g[:, h, bass.ds(b * L + r * CH, CH)], ALU.mult)
                last.then_inc(m2["yg"], 1)
                dve.wait_ge(m2["op"], b + 1)
                nc.vector.tensor_tensor(xs(b * L, L), bk45[:, :], xs(b * L, L), ALU.add).then_inc(m2["xupd"], 1)

        def ssm2_pool(pool):
            with pool.Fori(0, B) as b:
                with pool.Fori(0, NS // 2) as pair:
                    for q in range(2):
                        k = b * NS + pair * 2 + q
                        pool.wait_ge(m2["Cs"], k + 1 + FREE)
                        for h in range(HV):
                            pool.wait_ge(scanned[h], k + 1 + FREE)
                            pool.wait_ge(reduced[h], k + FREE)
                            nc.gpsimd.tensor_tensor(hC[:, h, :], hst[q][:, h, :], Cs[:, q, :], ALU.mult
                                                    ).then_inc(hC_done[h], 1)

        def ssm2_tensor(pe):
            pe.wait_ge(m1["u"], NC + FREE)
            with pe.Fori(0, B) as b:
                pe.wait_ge(m2["xupd"], b + FREE)
                for r in range(CPB):
                    for h in range(HV):
                        last = nc.tensor.matmul(bk45[0:KS3 + RK, r * CH:(r + 1) * CH], wx[:, h, :],
                                                u[:, h, bass.ds(b * L + r * CH, CH)], start=(h == 0), stop=(h == HV - 1))
                last.then_inc(m2["xp"], 1)
                pe.wait_ge(m2["xd"], b + 1)
                for h in range(HV):
                    for r in range(CPB):
                        last = nc.tensor.matmul(bank[h * CPB + r][:, :], wdt[KS3:KS3 + RK, h * P:(h + 1) * P],
                                                xd[KS3:KS3 + RK, r * CH:(r + 1) * CH], start=True, stop=True)
                last.then_inc(m2["dt"], 1)
                pe.wait_ge(m2["r3"], b + 1)
                pe.wait_ge(m2["delta"], b + 1)
                for h in range(HV):
                    for r in range(CPB):
                        nc.tensor.matmul(bank[h * CPB + r][:, :], diagD[:, h, :], u[:, h, bass.ds(b * L + r * CH, CH)],
                                         start=True, stop=False, skip_group_check=True)

                def spread_B(n):
                    k = b * NS + n
                    pe.wait_ge(m2["mul"], k * HV + FREE)
                    for r in range(CPB):
                        last = nc.tensor.matmul(bk45[:, r * CH:(r + 1) * CH], sel[:, n, :], s3[:, r * CH:(r + 1) * CH],
                                                start=True, stop=True)
                    last.then_inc(m2["B"], 1)

                def spread_C(n):
                    k = b * NS + n
                    pe.wait_ge(m2["Cs"], k + FREE)
                    for r in range(CPB):
                        last = nc.tensor.matmul(bk67[:, r * CH:(r + 1) * CH], sel[:, n + NS, :],
                                                s3[:, r * CH:(r + 1) * CH], start=True, stop=True)
                    last.then_inc(m2["C"], 1)

                def reduce(n, h):
                    pe.wait_ge(hC_done[h], b * NS + n + 1 + FREE)
                    for r in range(CPB):
                        last = nc.tensor.matmul(bank[h * CPB + r][:, :], ident[:, :], hC[:, h, r * CH:(r + 1) * CH],
                                                start=False, stop=True, skip_group_check=True)
                    last.then_inc(reduced[h], 1)

                for n in range(2):
                    spread_B(n)
                    spread_C(n)
                with pe.Fori(2, NS) as n:
                    reduce(n - 2, 0)
                    spread_B(n)
                    reduce(n - 2, 1)
                    spread_C(n)
                for n in range(NS - 2, NS):
                    for h in range(HV):
                        reduce(n, h)
                pe.wait_ge(m2["yg"], b + 1)
                for t in range(TPB):
                    o = bk45[:, t * P:(t + 1) * P]
                    nc.tensor.matmul(o, ones[0:1, :], bop[0:1, :], start=True, stop=False)
                    for h in range(HV):
                        last = nc.tensor.matmul(o, hC[:, h, t * P:(t + 1) * P], wop[:, h, :],
                                                start=False, stop=(h == HV - 1))
                last.then_inc(m2["op"], 1)

        def ssm2_scalar(act):
            nc.scalar.preload_act_table_set("natural_log_exp_and_others")
            with act.Fori(0, B) as b:
                act.wait_ge(m2["xp"], b + 1)
                nc.scalar.copy(hi3[:, :], bk45[0:KS3, :])
                nc.scalar.copy(xd[KS3:KS3 + RK, :], bk45[KS3:KS3 + RK, :]).then_inc(m2["xd"], 1)
                act.wait_ge(m2["dt"], b + 1)
                for h in range(HV):
                    for r in range(CPB):
                        last = nc.scalar.activation(ea[:, h, r * CH:(r + 1) * CH], bank[h * CPB + r][:, :], ACT.Abs,
                                                    bias=bdt[:, h:h + 1])
                last.then_inc(m2["ea"], 1)
                act.wait_ge(m2["ea"], b + 1)
                nc.scalar.activation(eb[:, :, :], ea[:, :, :], ACT.Exp, scale=-1.0).then_inc(m2["eb"], 1)
                act.wait_ge(m2["eb"], b + 1)
                nc.scalar.activation(du[:, :, :], eb[:, :, :], ACT.Ln, bias=1.0).then_inc(m2["ln"], 1)
                act.wait_ge(m2["delta"], b + 1)
                with act.Fori(0, NS // 2) as pair:
                    for q in range(2):
                        n = pair * 2 + q
                        k = b * NS + n

                        for h in range(HV):
                            act.wait_ge(scanned[h], k - 1 + FREE)
                            nc.scalar.activation(dA[q][:, h, :], delta[:, h, :], ACT.Exp,
                                                 scale=aneg[:, bass.ds(n + h * NS, 1)]).then_inc(dA_done[h], 1)
                        act.wait_ge(m2["C"], k + 1)
                        for h in range(HV):
                            act.wait_ge(hC_done[h], k - 1 + FREE)
                        nc.scalar.copy(Cs[:, q, :], bk67[:, :]).then_inc(m2["Cs"], 1)

        def weights_vector(dve):
            dve.wait_ge(w_in, 16 * len(loads))
            link = stepper(dve, set_dve_step, 0)
            nc.vector.tensor_reduce(asum[:, 0:1], wup[:, :], AX.X, ALU.add, apply_absolute_value=True)
            link(nc.vector.tensor_reduce(asum[:, 1:2], wdn[:, :, :], AX.XY, ALU.add, apply_absolute_value=True))
            dve.wait_ge(set_act, 1)
            nc.vector.tensor_scalar(aneg[:, :], aneg[:, :], -1.0, None, ALU.mult)
            for h in range(HV):
                nc.vector.tensor_scalar(diagD[:, h, :], ident[:, :], dpar[:, h:h + 1], None, ALU.mult)
            dve.wait_ge(set_pe, 1)
            nc.vector.tensor_scalar(thr[:, 0:2], psG[:, 0:2], 0.5 / (DFF * D), None, ALU.mult)
            link(nc.vector.tensor_scalar(thr[:, 2:4], psG[:, 0:2], -0.5 / (DFF * D), None, ALU.mult))
            for i, w in enumerate((wup[:, :], wdn[:, :, :].rearrange("p k n -> p (k n)"))):
                link(nc.vector.tensor_scalar(aw[:, :], w, thr[:, i:i + 1], None, ALU.is_gt))
                link(nc.vector.scalar_tensor_tensor(out=w, in0=w, scalar=thr[:, 2 + i:3 + i], in1=aw[:, :],
                                                    op0=ALU.is_lt, op1=ALU.subtract))
                last = nc.vector.tensor_scalar(w, w, -1.0, None, ALU.mult)
            last.then_inc(set_dve, 1)

        credited = [m1["xb"], m1["u"], m1["g"], m2["xupd"], m2["mul"], m2["Cs"]] + scanned + hC_done + reduced
        for f in (moe0, moe1, ter0, ter1):
            credited += [f.xupd, f.ssq if f.ternary else f.topd]

        first_loads = [
            (wg[:, :], Wg), (w1s[:, :], w1), (w2s[:, :, :], w2.rearrange("(k p) n -> p k n", p=P)),
        ]
        loads = [
            (wqkv[:, :], w_qkvT), (wo[:, :], w_outT), (bo[:, :], b_out.rearrange("(o n) -> o n", o=1)),
            (wup[:, :], upT), (wdn[:, :, :], downT.rearrange("(k p) n -> p k n", p=P)),
            (win[:, :], in_wT), (bin_[:, :], in_b),
            (cw[:, :, :], conv_w.rearrange("(h p) k -> p h k", p=P)), (cb[:, :], conv_b),
            (wdt[KS3:KS3 + RK, :], dt_wT), (bdt[:, :], dt_b),
            (alog[:, :].rearrange("p (h n) -> p h n", h=HV), A_log.rearrange("(h p) n -> p h n", p=P)),
            (dpar[:, :], D_param),
            (wop[:, :, :], op_wT.rearrange("(h p) n -> p h n", p=P)), (bop[:, :], op_b.rearrange("(o n) -> o n", o=1)),
        ]
        xpv = xp_wT.rearrange("(h p) n -> p h n", p=P)
        for r in range(3):
            loads.append((wx[:, :, r * 2 * NS:(r + 1) * 2 * NS], xpv[:, :, RK:RK + 2 * NS]))
        loads.append((wx[:, :, KS3:KS3 + RK], xpv[:, :, 0:RK]))

        block = ctx.enter_context(nc.Block())

        @block.sync
        def _(sp):
            for c in range(NC):
                sp.dma_start(x[:, c * CH:(c + 1) * CH].rearrange("p (t d) -> p t d", d=D),
                             x_src[:, c * TPC:(c + 1) * TPC, :]).then_inc(x_inp, 16)
            for dst, src in loads:
                sp.dma_start(dst, src).then_inc(w_in, 16)
            for s in credited:
                sp.sem_inc(s, FREE)
            for c in range(NC):
                sp.wait_ge(ter1.xupd, c + 1 + FREE)
                sp.dma_start(x_dst[:, c * TPC:(c + 1) * TPC, :],
                             x[:, c * CH:(c + 1) * CH].rearrange("p (t d) -> p t d", d=D)).then_inc(out_done, 16)
            sp.wait_ge(out_done, 16 * NC)

        @block.gpsimd
        def _(pool):
            link = stepper(pool, set_pool_step, 0)

            def select(t, op, fill, base, pattern, mult):
                link(nc.gpsimd.affine_select(out=t, in_=t, compare_op=op, fill=fill, base=base, pattern=pattern,
                                             channel_multiplier=mult))

            link(nc.gpsimd.memset(lnpow[:, 0:TPC], -0.5))
            link(nc.gpsimd.memset(lnpow[:, TPC:], 0.5))
            link(nc.gpsimd.memset(half[:, :], 0.5))
            link(nc.gpsimd.memset(lneps[:, :], LN_EPS))
            link(nc.gpsimd.memset(zeros[:, :], 0.0))
            link(nc.gpsimd.memset(ident[:, :], 0.0))
            select(ident[:, :], ALU.not_equal, 1.0, 0, [[-1, P]], 1)
            nc.gpsimd.memset(ones[:, :], 1.0).then_inc(set_pool, 1)
            ffn_pool(pool, moe0)

            link(nc.gpsimd.memset(identb[:, :], 0.0))
            select(identb[:, :], ALU.not_equal, 1.0, 0, [[-1, P]], 1)
            link(nc.gpsimd.memset(qmask[:, :], HD ** -0.5))
            for j in range(JG):
                select(qmask[32 * j:32 * j + 32, :], ALU.is_ge, 0.0, 0, [[-HD, HPG]], 1)
            for j in range(JG):
                select(qmask[32 * j:32 * j + 32, :], ALU.is_ge, 0.0, HD - 1, [[HD, HPG]], -1)
            link(nc.gpsimd.memset(mask[:, :, :], 0.0))
            for s in range(2):
                select(mask[64 * s:64 * s + 64, :, :], ALU.is_gt, MASKED, 0, [[0, NT], [1, P]], -1)
            for s in range(2):
                select(mask[64 * s:64 * s + 64, :, :], ALU.is_ge, MASKED, 64, [[0, NT], [-1, P]], 1)
            for b in range(B):
                link(nc.gpsimd.memset(mask[0:64, b * TPB, 0:64], MASKED))
            link(nc.gpsimd.memset(xw[:, :], 0.0))
            link(nc.gpsimd.memset(kT[:, :], 0.0))
            nc.gpsimd.memset(va[:, :, :, :], 1.0).then_inc(set_attn, 1)
            attn_pool(pool)

            link(nc.gpsimd.memset(xb[:, :, :, :], 0.0))
            link(nc.gpsimd.memset(sel[:, :, :], 0.0))
            for r in range(2):
                select(sel[:, :, :], ALU.not_equal, 1.0, -2 * NS * r, [[-1, 2 * NS], [0, P]], 1)
            nc.gpsimd.affine_select(out=sel[:, :, :], in_=sel[:, :, :], compare_op=ALU.not_equal, fill=1.0,
                                    base=-4 * NS, pattern=[[-1, 2 * NS], [0, P]],
                                    channel_multiplier=1).then_inc(set_ssm, 1)
            ffn_pool(pool, moe1)
            ffn_pool(pool, ter0)
            ssm1_pool(pool)
            ssm2_pool(pool)
            ffn_pool(pool, ter1)

        @block.scalar
        def _(act):
            for dst, src in first_loads:
                act.dma_start(dst, src).then_inc(w_moe, 16)
            act.preload_act_table(ACT.Exp)
            ffn_scalar(act, moe0)
            act.wait_ge(w_in, 16 * len(loads))
            nc.scalar.activation(aneg[:, :], alog[:, :], ACT.Exp).then_inc(set_act, 1)
            act.wait_ge(set_attn, 1)
            attn_scalar(act)
            ffn_scalar(act, moe1)
            ffn_scalar(act, ter0)
            act.wait_ge(set_ssm, 1)
            ssm1_scalar(act)
            ssm2_scalar(act)
            ffn_scalar(act, ter1)

        @block.vector
        def _(dve):
            dve.wait_ge(set_pool, 1)
            ffn_vector(dve, moe0, x_inp, 16 * NC)
            weights_vector(dve)
            attn_vector(dve)
            ffn_vector(dve, moe1, at["xupd"], NT)
            ffn_vector(dve, ter0, moe1.xupd, NC + FREE)
            ssm1_vector(dve)
            ssm2_vector(dve)
            ffn_vector(dve, ter1, m2["xupd"], B + FREE)

        @block.tensor
        def _(pe):
            pe.wait_ge(w_moe, 16 * len(first_loads))
            pe.wait_ge(set_pool, 1)
            ffn_tensor(pe, moe0)
            pe.wait_ge(set_dve_step, 1)
            nc.tensor.matmul(psG[:, 0:2], ones[:, :], asum[:, :], start=True, stop=True).then_inc(set_pe, 1)
            pe.wait_ge(set_dve, 1)
            pe.wait_ge(w_in, 16 * len(loads))
            pe.wait_ge(set_attn, 1)
            attn_tensor(pe)
            ffn_tensor(pe, moe1)
            ffn_tensor(pe, ter0)
            pe.wait_ge(set_ssm, 1)
            ssm1_tensor(pe)
            ssm2_tensor(pe)
            ffn_tensor(pe, ter1)


def kernel(**inputs):
    import numpy as _np
    import concourse.bacc as _bacc
    from concourse import mybir as _mybir
    from concourse.bass_utils import run_bass_kernel_spmd as _run

    def turned(name):
        return _np.ascontiguousarray(_np.asarray(inputs[name]).T)

    def plain(name):
        return _np.ascontiguousarray(inputs[name])

    def columns(name):
        return _np.ascontiguousarray(_np.asarray(inputs[name]).reshape(-1, P).T)

    conv = plain("L1_attn_conv_w")
    ins = [
        ("x", plain("L0_attn_x")), ("w_qkvT", turned("L0_attn_w_qkv")), ("w_outT", turned("L0_attn_w_out")),
        ("b_out", plain("L0_attn_b_out")), ("Wg", plain("L0_ffn_Wg")), ("w1", plain("L0_ffn_w1")),
        ("w2", plain("L0_ffn_w2")), ("in_wT", turned("L1_attn_in_proj_w")), ("in_b", columns("L1_attn_in_proj_b")),
        ("conv_w", conv.reshape(conv.shape[0], conv.shape[2])), ("conv_b", columns("L1_attn_conv_b")),
        ("xp_wT", turned("L1_attn_x_proj_w")), ("dt_wT", turned("L1_attn_dt_proj_w")),
        ("dt_b", columns("L1_attn_dt_proj_b")), ("A_log", plain("L1_attn_A_log")), ("D_param", columns("L1_attn_D_param")),
        ("op_wT", turned("L1_attn_out_proj_w")), ("op_b", plain("L1_attn_out_proj_b")),
        ("upT", turned("L1_ffn_w_up")), ("downT", turned("L1_ffn_w_down")),
    ]
    nc = _bacc.Bacc("TRN2", target_bir_lowering=False, num_devices=1)
    arrays = {f"in_{n}_dram": a for n, a in ins}
    args = [nc.dram_tensor(f"in_{n}_dram", a.shape, _mybir.dt.from_np(a.dtype), kind="ExternalInput").ap()
            for n, a in ins]
    x0 = ins[0][1]
    args.append(nc.dram_tensor("out_dram", x0.shape, _mybir.dt.from_np(x0.dtype), kind="ExternalOutput").ap())
    macaron_kernel(nc, *args)
    r = _run(nc, [arrays], core_ids=[0])
    return r.results[0]["out_dram"]
```
